# Optimizing a Trainium2 kernel written in Bass

```python
import numpy as np
import jax
import jax.numpy as jnp

def _softmax(x, axis=-1):
    return jax.nn.softmax(x, axis=axis)

def _gelu(x):
    return jax.nn.gelu(x, approximate=True)

def _silu(x):
    return jax.nn.silu(x)

def _sigmoid(x):
    return jax.nn.sigmoid(x)

def _layernorm(x, axis=-1, eps=1e-05):
    m = jnp.mean(x, axis=axis, keepdims=True)
    v = jnp.var(x, axis=axis, keepdims=True)
    return (x - m) / jnp.sqrt(v + eps)

def _scatter_add(tgt, idx, src, axis=0):
    return tgt.at[idx].add(src)

def _segment_sum(src, seg, n):
    return jax.ops.segment_sum(src, seg, n)
kernel_name = 'mk_gnn_resnorm_d2_gnn_r32_57d555'

def setup_inputs(seed: int=0):
    np.random.seed(seed)
    _w = jnp.asarray

    def _rec_inputs():
        import jax
        import jax.numpy as jnp
        _gk = jax.random.key(seed)
        x = -0.0001006 + 1 * jax.random.normal(jax.random.fold_in(_gk, 1), (3125, 96), jnp.float32)
        _s = jax.random.randint(jax.random.fold_in(_gk, 2), (50000,), 0, 3125, jnp.int32)
        _d = jax.random.randint(jax.random.fold_in(_gk, 3), (50000,), 0, 3125, jnp.int32)
        _loop = jnp.arange(3125, dtype=jnp.int32)
        src = jnp.concatenate([_s, _d, _loop])
        dst = jnp.concatenate([_d, _s, _loop])
        _o = jnp.argsort(dst, stable=True)
        src = src[_o]
        dst = dst[_o]
        edge_attr_32 = 0.000196303 + 1.00016 * jax.random.normal(jax.random.fold_in(_gk, 12), (103125, 32), jnp.float32)
        edge_weight = jax.random.uniform(jax.random.fold_in(_gk, 14), (103125,), jnp.float32, 0.0, 1)
        return (x, src, dst, edge_attr_32, edge_weight)
    x, src, dst, edge_attr_32, edge_weight = _rec_inputs()

    def _L0_gnn_setup():
        import jax, jax.numpy as jnp
        import numpy as np
        N_NODES = 50000
        N_EDGES = 25000
        EMB = 96
        LAYER_NUM = 3
        key = jax.random.key(seed)
        k1, k2, k3, k4 = jax.random.split(key, 4)
        X = jax.random.normal(k1, (N_NODES, EMB), dtype=jnp.float32)
        vals = jax.random.uniform(k2, (N_EDGES,), dtype=jnp.float32)
        rows = jax.random.randint(k3, (N_EDGES,), 0, N_NODES, dtype=jnp.int64)
        cols = jax.random.randint(k4, (N_EDGES,), 0, N_NODES, dtype=jnp.int64)
        return {'X': X, 'vals': vals, 'rows': rows, 'cols': cols}
    _L0_gnn_all = _L0_gnn_setup()
    _L0_gnn_in = {k: v for k, v in _L0_gnn_all.items() if k in ()}
    del _L0_gnn_all

    def _L1_gnn_setup():
        import jax, jax.numpy as jnp
        import numpy as np
        N, E = (50000, 25000)
        DIN = DOUT = 96
        DE = 32

        def _egnn_conv(x, src, dst, edge_attr, W_msg, W_edge, W_root, b):
            msg = x[src] @ W_msg + edge_attr @ W_edge
            agg = jax.ops.segment_max(msg, dst, num_segments=x.shape[0])
            agg = jnp.where(jnp.isneginf(agg), 0.0, agg)
            return agg + x @ W_root + b
        key = jax.random.key(seed)
        ks = jax.random.split(key, 10)
        rn = lambda k, sh, sc: jax.random.normal(k, sh, jnp.float32) * sc
        return {'X': rn(ks[0], (N, DIN), 1.0), 'edge_index': jax.random.randint(ks[1], (2, E), 0, N, jnp.int32), 'edge_attr': rn(ks[2], (E, DE), 1.0), 'W1_msg': rn(ks[3], (DIN, DOUT), DIN ** (-0.5)), 'W1_edge': rn(ks[4], (DE, DOUT), DE ** (-0.5)), 'W1_root': rn(ks[5], (DIN, DOUT), DIN ** (-0.5)), 'b1': jnp.zeros((DOUT,), jnp.float32), 'W2_msg': rn(ks[6], (DOUT, DOUT), DOUT ** (-0.5)), 'W2_edge': rn(ks[7], (DE, DOUT), DE ** (-0.5)), 'W2_root': rn(ks[8], (DOUT, DOUT), DOUT ** (-0.5)), 'b2': jnp.zeros((DOUT,), jnp.float32)}
    _L1_gnn_all = _L1_gnn_setup()
    _L1_gnn_in = {k: v for k, v in _L1_gnn_all.items() if k in ('W1_msg', 'W1_edge', 'W1_root', 'b1', 'W2_msg', 'W2_edge', 'W2_root', 'b2')}
    del _L1_gnn_all
    return {'x': x, 'src': src, 'dst': dst, 'edge_attr_32': edge_attr_32, 'edge_weight': edge_weight, 'L1_gnn_W1_msg': _L1_gnn_in['W1_msg'], 'L1_gnn_W1_edge': _L1_gnn_in['W1_edge'], 'L1_gnn_W1_root': _L1_gnn_in['W1_root'], 'L1_gnn_b1': _L1_gnn_in['b1'], 'L1_gnn_W2_msg': _L1_gnn_in['W2_msg'], 'L1_gnn_W2_edge': _L1_gnn_in['W2_edge'], 'L1_gnn_W2_root': _L1_gnn_in['W2_root'], 'L1_gnn_b2': _L1_gnn_in['b2']}

def reference(x, src, dst, edge_attr_32, edge_weight, L1_gnn_W1_msg, L1_gnn_W1_edge, L1_gnn_W1_root, L1_gnn_b1, L1_gnn_W2_msg, L1_gnn_W2_edge, L1_gnn_W2_root, L1_gnn_b2):
    import jax
    import jax.numpy as jnp

    def _L0_gnn_ref(X, vals, rows, cols):
        import jax, jax.numpy as jnp
        import numpy as np
        N_NODES = 50000
        N_EDGES = 25000
        EMB = 96
        LAYER_NUM = 3
        N = X.shape[0]
        ego = X
        acc = X
        for _ in range(LAYER_NUM):
            msgs = vals[:, None] * ego[cols]
            agg = jax.ops.segment_sum(msgs, rows, num_segments=N)
            ego = agg + agg * ego
            acc = acc + ego
        return acc / jnp.asarray(LAYER_NUM + 1, dtype=X.dtype)

    def _L1_gnn_ref(X, edge_index, edge_attr, W1_msg, W1_edge, W1_root, b1, W2_msg, W2_edge, W2_root, b2):
        import jax, jax.numpy as jnp
        import numpy as np
        N, E = (50000, 25000)
        DIN = DOUT = 96
        DE = 32

        def _egnn_conv(x, src, dst, edge_attr, W_msg, W_edge, W_root, b):
            msg = x[src] @ W_msg + edge_attr @ W_edge
            agg = jax.ops.segment_max(msg, dst, num_segments=x.shape[0])
            agg = jnp.where(jnp.isneginf(agg), 0.0, agg)
            return agg + x @ W_root + b
        src, dst = (edge_index[0], edge_index[1])
        c1 = jax.nn.leaky_relu(_egnn_conv(X, src, dst, edge_attr, W1_msg, W1_edge, W1_root, b1))
        c2 = jax.nn.leaky_relu(_egnn_conv(c1, src, dst, edge_attr, W2_msg, W2_edge, W2_root, b2))
        return c2
    edge_index = jnp.stack([src, dst])
    x = _layernorm(x + _L0_gnn_ref(x, edge_weight, src, dst), axis=-1)
    x = _layernorm(x + _L1_gnn_ref(x, edge_index, edge_attr_32, L1_gnn_W1_msg, L1_gnn_W1_edge, L1_gnn_W1_root, L1_gnn_b1, L1_gnn_W2_msg, L1_gnn_W2_edge, L1_gnn_W2_root, L1_gnn_b2), axis=-1)
    return x

_drawn_inputs = setup_inputs


def setup_inputs(seed=0):
    import zlib

    import numpy as np

    out = dict(_drawn_inputs(seed))
    spreads = {'L1_gnn_b1': (0.0, 0.271), 'L1_gnn_b2': (0.0, 0.287)}
    factors = {}
    for name, (base, spread) in spreads.items():
        noise = np.random.default_rng([zlib.crc32(name.encode()), seed]).standard_normal(out[name].shape)
        drawn = base * np.exp(spread * noise) if base else spread * noise
        out[name] = jnp.asarray(drawn.astype(out[name].dtype))
    for name, factor in factors.items():
        out[name] = (out[name] * factor).astype(out[name].dtype)
    return out
```

```python
from contextlib import ExitStack

import concourse.bass as bass
from concourse import mybir

F32, BF16, I32 = mybir.dt.float32, mybir.dt.bfloat16, mybir.dt.int32
ALU, ACT, AX = mybir.AluOpType, mybir.ActivationFunctionType, mybir.AxisListType

P = 128
N, D, E, DE = 3125, 96, 103125, 32
ROUNDS = 3
EPS = 1e-5
SLOPE = 0.01

NB = 128
NA = -(-N // NB)
SPAD = NA * NB
NP = 125
NT = N // NP
G = NP // NA
NG = N // G
GT = NG // NP
GK = NP // G

CH = 512
NC = -(-E // CH)
ROW = 32
EW = 26 * ROW
EP = P * EW
PROWS = EP // ROW
WR = 8
WIN = WR * ROW
HALF = WIN // P
STEPS = GK * HALF
DPAD = 4000
FAR = -3.3e38


def full_rows(width):
    return E // width, E % width


class Chain:

    def __init__(self, eng, sem):
        self.eng, self.sem, self.n = eng, sem, 0

    def __call__(self, ins):
        self.n += 1
        ins.then_inc(self.sem, 1)
        self.eng.wait_ge(self.sem, self.n)


class Mem:
    pass


def persistent(nc, ctx, m):
    def sb(name, shape, dt=F32):
        return ctx.enter_context(nc.sbuf_tensor(name, shape, dt))

    m.ident = sb("ident", [P, P])
    m.iota = sb("iota", [P, P])
    m.src_idx = sb("src_idx", [P, EP // P], I32)
    m.x = sb("x_nat", [NP, NT, D])
    m.end_idx = sb("end_idx", [NP, NT], I32)
    m.zero = sb("zero_row", [NP, D])
    m.eps = sb("eps", [NP, 1])

    def dram(name, shape, dt=F32):
        return nc.dram_tensor(name, shape, dt, kind="Internal").ap()

    m.packed = dram("packed", (PROWS, 3 * ROW))
    m.mask = dram("mask", (P, EW), BF16)
    m.ends = dram("ends", (1 + SPAD,), I32)
    m.adj = dram("adj", (N, SPAD))
    m.y = dram("y_rows", (N, D))
    m.seg = dram("seg", (NC * CH + 1, D))


def phase_prepare(nc, m):
    with ExitStack() as ctx:
        def sb(name, shape, dt=F32):
            return ctx.enter_context(nc.sbuf_tensor(name, shape, dt))

        def sem(name):
            return ctx.enter_context(nc.semaphore(name))

        ramp = sb("ramp", [P, P], I32)
        dst = sb("dst", [P, EW], I32)
        src = sb("src", [P, EW], I32)
        wt = sb("wt", [P, EW])
        before = sb("before", [P, 1], I32)
        part = sb("part", [P, EW], I32)
        pack = sb("pack", [P, EW, 3])
        flag = sb("flag", [P, EW])
        maskb = sb("maskb", [P, EW], BF16)
        da = sb("da", [P, EW])
        db = sb("db", [P, EW])
        HT = 8
        oh_a = [sb(f"oh_a{k}", [P, HT, NA], BF16) for k in range(2)]
        oh_b = [sb(f"oh_b{k}", [P, HT, NB], BF16) for k in range(2)]
        cnt = sb("cnt", [NA, NB])
        run = sb("run", [NA, NB])
        zeros = sb("zeros", [NA, NB])
        ends_i = sb("ends_i", [NA, NB], I32)
        tri = sb("tri", [NA, NA])
        one0 = sb("one0", [1, 1], I32)
        hist = ctx.enter_context(nc.psum_tensor("hist", [NA, NB], F32))
        carry = ctx.enter_context(nc.psum_tensor("carry", [NA, 1], F32))

        s_const, s_ramp, s_fill, s_load, s_vec = (sem(n) for n in ("const", "ramp_rdy", "filled", "loaded", "vec"))
        s_packed, s_maskr, s_split = sem("packed_rdy"), sem("mask_rdy"), sem("split_rdy")
        s_oh, s_ohfree, s_hist = sem("onehots_rdy"), sem("onehots_free"), sem("hist_done")
        s_tot, s_carry, s_ends, s_out = sem("totals_rdy"), sem("carry_rdy"), sem("ends_rdy"), sem("stored")
        s_gz, s_order = sem("pool_chain"), sem("ordered_in")
        block = ctx.enter_context(nc.Block())
        full, rest = full_rows(EW)
        cfull, crest = full_rows(CH)
        LOADS = 9

        @block.sync
        def _(sp):
            sp.wait_ge(s_fill, 5)
            for buf, arr in ((dst, m.dst), (src, m.src), (wt, m.w)):
                sp.dma_start(buf[0:full, :], arr[0:full * EW].rearrange("(p e) -> p e", e=EW)).then_inc(s_load, 16)
                sp.dma_start(buf[full:full + 1, 0:rest], arr[full * EW:E].unsqueeze(0)).then_inc(s_load, 16)
            with nc.allow_non_contiguous_dma(reason="one neighbour per partition"):
                sp.dma_start(before[1:full + 1, :],
                             m.dst[0:full * EW].rearrange("(p e) -> p e", e=EW)[:, EW - 1:EW]).then_inc(s_load, 16)
            sp.dma_start(m.x[:, :, :], m.x_in.rearrange("(k p) d -> p k d", p=NP)).then_inc(s_load, 16)
            sp.dma_start(m.seg[NC * CH:NC * CH + 1, :], m.zero[0:1, :]).then_inc(s_load, 16)
            sp.wait_ge(s_packed, 3)
            sp.dma_start(m.packed.rearrange("(p r) c -> p (r c)", p=P),
                         pack[:, :, :].rearrange("p e c -> p (e c)")).then_inc(s_out, 16)
            sp.wait_ge(s_maskr, 1)
            sp.dma_start(m.mask, maskb[:, :]).then_inc(s_out, 16)
            sp.wait_ge(s_ends, 1)
            sp.dma_start(m.ends[1:1 + SPAD].rearrange("(a b) -> a b", b=NB), ends_i[:, :]).then_inc(s_out, 16)
            sp.dma_start(m.ends[0:1].unsqueeze(0), one0[:, :]).then_inc(s_out, 16)
            sp.wait_ge(s_out, 64)
            sp.wait_ge(s_load, 16 * LOADS)

        @block.gpsimd
        def _(g):
            nc.gpsimd.memset(m.src_idx[:, :], 0).then_inc(s_fill, 1)
            nc.gpsimd.iota(ramp[:, :], pattern=[[1, P]], base=0, channel_multiplier=0).then_inc(s_ramp, 1)
            nc.gpsimd.memset(m.ident[:, :], 0.0).then_inc(s_gz, 1)
            nc.gpsimd.memset(tri[:, :], 1.0).then_inc(s_gz, 1)
            g.wait_ge(s_gz, 2)
            nc.gpsimd.affine_select(out=m.ident[:, :], in_=m.ident[:, :], compare_op=ALU.not_equal, fill=1.0, base=0,
                                    pattern=[[-1, P]], channel_multiplier=1).then_inc(s_const, 1)
            nc.gpsimd.affine_select(out=tri[:, :], in_=tri[:, :], compare_op=ALU.is_gt, fill=0.0, base=0,
                                    pattern=[[1, NA]], channel_multiplier=-1).then_inc(s_const, 1)

        @block.scalar
        def _(act):
            act.wait_ge(s_fill, 5)
            idx = m.src_idx[:, :].rearrange("p (c j) -> p c j", j=4)
            act.dma_start(idx[:, 0:cfull, :],
                          m.src[0:cfull * CH].rearrange("(c p j) -> p c j", p=P, j=4)).then_inc(s_order, 16)
            act.dma_start(idx[0:crest // 4, cfull, :],
                          m.src[cfull * CH:E - crest % 4].rearrange("(p j) -> p j", j=4)).then_inc(s_order, 16)
            act.dma_start(idx[crest // 4:crest // 4 + 1, cfull, 0:crest % 4],
                          m.src[E - crest % 4:E].unsqueeze(0)).then_inc(s_order, 16)
            act.wait_ge(s_order, 16 * 3)

        @block.vector
        def _(v):
            link = Chain(v, s_vec)
            nc.vector.memset(dst[:, :], DPAD).then_inc(s_fill, 1)
            nc.vector.memset(src[:, :], 0).then_inc(s_fill, 1)
            nc.vector.memset(wt[:, :], 0.0).then_inc(s_fill, 1)
            nc.vector.memset(m.zero[:, :], 0.0)
            nc.vector.memset(m.eps[:, :], EPS)
            nc.vector.memset(one0[:, :], 0)
            nc.vector.memset(zeros[:, :], 0.0)
            nc.vector.memset(before[:, :], -1).then_inc(s_fill, 1)
            v.wait_ge(s_ramp, 1)
            link(nc.vector.tensor_copy(m.iota[:, :], ramp[:, :]))
            v.wait_ge(s_load, 16 * LOADS)
            link(nc.vector.tensor_scalar(part[:, :], dst[:, :], 7, None, ALU.arith_shift_right))
            link(nc.vector.tensor_copy(da[:, :], part[:, :]))
            link(nc.vector.tensor_scalar(part[:, :], dst[:, :], NB - 1, None, ALU.bitwise_and))
            link(nc.vector.tensor_copy(db[:, :], part[:, :]))
            link(nc.vector.tensor_scalar(part[:, :], src[:, :], NB - 1, None, ALU.bitwise_and))
            nc.vector.tensor_copy(pack[:, :, 0], part[:, :]).then_inc(s_packed, 1)
            v.wait_ge(s_packed, 1)
            link(nc.vector.tensor_scalar(part[:, :], src[:, :], 7, None, ALU.arith_shift_right))
            nc.vector.scalar_tensor_tensor(out=pack[:, :, 1], in0=dst[:, :], scalar=float(NA), in1=part[:, :],
                                           op0=ALU.mult, op1=ALU.add).then_inc(s_packed, 1)
            nc.vector.tensor_copy(pack[:, :, 2], wt[:, :]).then_inc(s_packed, 1)
            link(nc.vector.tensor_tensor(flag[:, 1:EW], dst[:, 1:EW], dst[:, 0:EW - 1], ALU.not_equal))
            link(nc.vector.tensor_tensor(flag[:, 0:1], dst[:, 0:1], before[:, :], ALU.not_equal))
            nc.vector.tensor_scalar(maskb[:, :], flag[:, :], FAR, None, ALU.mult).then_inc(s_maskr, 1)
            with v.Fori(0, EW // HT // 2) as i:
                for k in range(2):
                    v.wait_ge(s_ohfree, i * 2 + k + 1)
                    cols = bass.ds((i * 2 + k) * HT, HT)
                    nc.vector.tensor_tensor(oh_a[k][:, :, :], m.iota[:, 0:NA].unsqueeze(1).to_broadcast([P, HT, NA]),
                                            da[:, cols].unsqueeze(2).to_broadcast([P, HT, NA]),
                                            ALU.is_equal).then_inc(s_oh, 1)
                    nc.vector.tensor_tensor(oh_b[k][:, :, :], m.iota[:, :].unsqueeze(1).to_broadcast([P, HT, NB]),
                                            db[:, cols].unsqueeze(2).to_broadcast([P, HT, NB]),
                                            ALU.is_equal).then_inc(s_oh, 1)
            v.wait_ge(s_hist, 1)
            link(nc.vector.tensor_copy(cnt[:, :], hist[:, :]))
            link(nc.vector.tensor_tensor_scan(run[:, :], cnt[:, :], zeros[:, :], 0.0, ALU.add, ALU.add))
            v.sem_inc(s_tot, 1)
            v.wait_ge(s_carry, 1)
            nc.vector.tensor_scalar(ends_i[:, :], run[:, :], carry[:, 0:1], None, ALU.add).then_inc(s_ends, 1)

        @block.tensor
        def _(pe):
            pe.sem_inc(s_ohfree, 2)
            n_slots = EW // HT

            def count(k, slot, first, last):
                pe.wait_ge(s_oh, (slot + 1) * 2)
                for t in range(HT):
                    mm = nc.tensor.matmul(hist[:, :], oh_a[k][:, t, :], oh_b[k][:, t, :],
                                          start=first and t == 0, stop=last and t == HT - 1)
                mm.then_inc(s_ohfree, 1)

            count(0, 0, True, False)
            count(1, 1, False, False)
            with pe.Fori(1, n_slots // 2 - 1) as i:
                for k in range(2):
                    count(k, i * 2 + k, False, False)
            count(0, n_slots - 2, False, False)
            count(1, n_slots - 1, False, True)
            pe.wait_ge(s_ohfree, n_slots + 2)
            pe.sem_inc(s_hist, 1)
            pe.wait_ge(s_tot, 1)
            pe.wait_ge(s_const, 2)
            nc.tensor.matmul(carry[:, :], tri[:, :], run[:, NB - 1:NB], start=True, stop=True).then_inc(s_carry, 1)


def phase_adjacency(nc, m):
    with ExitStack() as ctx:
        def sb(name, shape, dt=F32):
            return ctx.enter_context(nc.sbuf_tensor(name, shape, dt))

        def sem(name):
            return ctx.enter_context(nc.semaphore(name))

        lo = sb("lo", [NP, GT], I32)
        rowi = sb("rowi", [NP, GT], I32)
        widx = sb("widx", [NP, GT, WR], I32)
        nb = sb("nb", [NP, NT], I32)
        ne = sb("ne", [NP, NT], I32)
        has = sb("has", [NP, NT])
        last = sb("last", [NP, NT])
        win = sb("win", [NP, GT, WR * 3 * ROW])
        goff_i = sb("goff_i", [P, NG], I32)
        goff = sb("goff", [P, NG])
        cols = [sb(f"col{c}", [P, NG * HALF]) for c in range(3)]
        RING = 10
        oh_m = [sb(f"oh_m{r}", [P, NP]) for r in range(RING)]
        oh_w = [sb(f"oh_w{r}", [P, NB]) for r in range(RING)]
        rows = sb("rows", [NP, 2, GK, NB])
        pt = [ctx.enter_context(nc.psum_tensor(f"pt{k}", [P, 512], F32)) for k in range(8)]

        s_ld, s_dv, s_gidx, s_gidx2, s_win = sem("ends_in"), sem("dve_chain"), sem("goff_rdy"), sem("widx_rdy"), sem("win_in")
        s_tr, s_ev, s_cols = sem("slots_up"), sem("slots_out"), sem("cols_rdy")
        s_ohr, s_free, s_done, s_evd = sem("oh_rdy"), sem("oh_free"), sem("bank_done"), sem("bank_free")
        s_rfree, s_rr = [sem(f"rows_stored{k}") for k in range(2)], sem("rows_rdy")
        block = ctx.enter_context(nc.Block())
        BANKS = [4] * 6 + [1]
        NBK = len(BANKS)
        CUT = 112

        @block.sync
        def _(sp):
            with nc.allow_non_contiguous_dma(reason="one count per group or node"):
                sp.dma_start(lo[:, :], m.ends[0:N].rearrange("(t p g) -> p t g", p=NP, g=G)[:, :, 0]).then_inc(s_ld, 16)
                sp.dma_start(nb[:, :], m.ends[0:N].rearrange("(k p) -> p k", p=NP)).then_inc(s_ld, 16)
                sp.dma_start(ne[:, :], m.ends[1:1 + N].rearrange("(k p) -> p k", p=NP)).then_inc(s_ld, 16)
            out = m.adj.rearrange("d (a b) -> (d a) b", b=NB).rearrange("(q m) b -> m q b", m=NP)

            def store(k, t, parity):
                at = t * GK if isinstance(t, int) else sp.snap(t * GK)
                sp.wait_ge(s_rr, (t + 1) * NBK)
                for p0, p1 in ((0, CUT), (CUT, NP)):
                    sp.dma_start(out[p0:p1, bass.ds(at, GK), :],
                                 rows[p0:p1, parity, :, :]).then_inc(s_rfree[parity], 16)

            with sp.Fori(0, NT // 2) as i:
                for k in range(2):
                    store(k, i * 2 + k, k)
            store(0, NT - 1, 0)
            sp.wait_ge(s_rfree[0], 32 * (NT // 2 + 1))
            sp.wait_ge(s_rfree[1], 32 * (NT // 2))

        @block.gpsimd
        def _(g):
            nc.gpsimd.iota(goff_i[:, :], pattern=[[NP, NG]], base=0, channel_multiplier=0).then_inc(s_gidx, 1)
            g.wait_ge(s_gidx2, 1)
            for t in range(GT):
                for r in range(WR):
                    g.indirect_dma_start(win[:, t, r * 3 * ROW:(r + 1) * 3 * ROW], None, m.packed,
                                         bass.IndirectOffsetOnAxis(ap=widx[:, t, r:r + 1], axis=0)).then_inc(s_win, 16)
            g.wait_ge(s_win, 16 * GT * WR)

        @block.vector
        def _(v):
            link = Chain(v, s_dv)
            v.wait_ge(s_ld, 48)
            link(nc.vector.tensor_scalar(rowi[:, :], lo[:, :], 5, None, ALU.arith_shift_right))
            for r in range(WR):
                w = nc.vector.tensor_scalar(widx[:, :, r], rowi[:, :], float(r), None, ALU.add)
            w.then_inc(s_gidx2, 1)
            zero_row = float(NC * CH)
            link(nc.vector.tensor_tensor(has[:, :], ne[:, :], nb[:, :], ALU.is_gt))
            link(nc.vector.tensor_scalar(last[:, :], ne[:, :], -1.0 - zero_row, None, ALU.add))
            link(nc.vector.tensor_tensor(last[:, :], last[:, :], has[:, :], ALU.mult))
            link(nc.vector.tensor_scalar(m.end_idx[:, :], last[:, :], zero_row, None, ALU.add))
            v.wait_ge(s_gidx, 1)
            link(nc.vector.tensor_copy(goff[:, :], goff_i[:, :]))
            n = 0
            for t in range(GT):
                for h in range(HALF):
                    for c in range(3):
                        n += 1
                        v.wait_ge(s_tr, n)
                        dst = cols[c][:, :].rearrange("p (t q h) -> p t h q", t=GT, h=HALF)[:, t, h, :]
                        up = pt[(n - 1) % 4][:, 0:NP]
                        if c == 1:
                            nc.vector.tensor_tensor(dst, up, goff[:, t * NP:(t + 1) * NP], ALU.subtract).then_inc(s_ev, 1)
                        else:
                            nc.vector.tensor_copy(dst, up).then_inc(s_ev, 1)
            v.wait_ge(s_ev, n)
            with v.Fori(0, NT) as i:
                for s in range(STEPS):
                    r = s % RING
                    v.wait_ge(s_free, i * STEPS + s + 1)
                    c = bass.ds(i * STEPS + s, 1)
                    nc.vector.tensor_scalar(oh_m[r][:, :], m.iota[:, 0:NP], cols[1][:, c], None,
                                            ALU.is_equal).then_inc(s_ohr, 1)
                    nc.vector.tensor_scalar(oh_w[r][:, :], m.iota[:, :], cols[0][:, c], cols[2][:, c],
                                            ALU.is_equal, ALU.mult).then_inc(s_ohr, 1)

        @block.scalar
        def _(act):
            def evict(t, parity):
                q = 0
                for k, n in enumerate(BANKS):
                    act.wait_ge(s_done, t * NBK + k + 1)
                    nc.scalar.copy(rows[:, parity, q:q + n, :], pt[k][0:NP, 0:n * NB].rearrange("p (q b) -> p q b", b=NB))\
                        .then_inc(s_rr, 1)
                    q += n

            for t in range(2):
                evict(t, t)
            with act.Fori(1, NT // 2) as i:
                for k in range(2):
                    act.wait_ge(s_rfree[k], i * 32)
                    evict(i * 2 + k, k)
            act.wait_ge(s_rfree[0], 32 * (NT // 2))
            evict(NT - 1, 0)

        @block.tensor
        def _(pe):
            pe.sem_inc(s_free, RING)
            n = 0
            pe.wait_ge(s_win, 16 * GT * WR)
            for t in range(GT):
                for h in range(HALF):
                    wv = win[:, t, :].rearrange("p (s c) -> p c s", c=3)
                    for c in range(3):
                        if n >= 4:
                            pe.wait_ge(s_ev, n - 3)
                        nc.tensor.transpose(pt[n % 4][:, 0:NP], wv[:, c, P * h:P * h + P],
                                            m.ident[0:NP, 0:NP]).then_inc(s_tr, 1)
                        n += 1
            pe.wait_ge(s_ev, n)

            def tile_of_groups(t, first):
                s = 0
                for k, groups in enumerate(BANKS):
                    if not first:
                        pe.wait_ge(s_rr, (t - 1) * NBK + k + 1)
                    for q in range(groups):
                        for h in range(HALF):
                            r = s % RING
                            pe.wait_ge(s_ohr, (t * STEPS + s + 1) * 2)
                            mm = nc.tensor.matmul(pt[k][0:NP, q * NB:(q + 1) * NB], oh_m[r][:, :], oh_w[r][:, :],
                                                  start=h == 0, stop=h == HALF - 1)
                            mm.then_inc(s_free, 1)
                            s += 1
                    pe.wait_ge(s_free, t * STEPS + s + RING)
                    pe.sem_inc(s_done, 1)

            tile_of_groups(0, True)
            with pe.Fori(1, NT) as i:
                tile_of_groups(i, False)


def layer_norm(nc, link, x, tmp, stats, out, eps, s_go, s_back, v):
    shape = [NP, NT, D]
    mean, var = stats[:, 0, :], stats[:, 1, :]
    link(nc.vector.reduce_sum(mean, x, AX.X))
    link(nc.vector.tensor_scalar(mean, mean, 1.0 / D, None, ALU.mult))
    link(nc.vector.tensor_tensor(x, x, mean.unsqueeze(2).to_broadcast(shape), ALU.subtract))
    link(nc.vector.tensor_tensor(tmp, x, x, ALU.mult))
    link(nc.vector.reduce_sum(var, tmp, AX.X))
    nc.vector.tensor_scalar(var, var, 1.0 / D, None, ALU.mult).then_inc(s_go, 1)
    v.wait_ge(s_back, 1)
    link(nc.vector.reciprocal(var, var))
    link(nc.vector.tensor_tensor(out, x, var.unsqueeze(2).to_broadcast(shape), ALU.mult))


def phase_propagate(nc, m):
    with ExitStack() as ctx:
        def sb(name, shape, dt=F32):
            return ctx.enter_context(nc.sbuf_tensor(name, shape, dt))

        def sem(name):
            return ctx.enter_context(nc.semaphore(name))

        UK = 5
        ego = sb("ego", [NP, NT, D])
        acc = sb("acc", [NP, NT, D])
        tmp = sb("tmp", [NP, NT, D])
        stats = sb("stats", [NP, 2, NT])
        slot = [sb(f"slot{k}", [NP, D]) for k in range(UK)]
        at = [sb(f"at{k}", [NP, SPAD]) for k in range(UK)]
        agg_t = sb("agg_t", [D, SPAD])
        pa = [ctx.enter_context(nc.psum_tensor(f"pa{k}", [P, 512], F32)) for k in range(8)]
        s_at = [sem(f"adj_in{k}") for k in range(UK)]
        s_afree, s_init, s_slot, s_agg, s_out, s_tr, s_upd, s_ln, s_rt, s_dv = (
            sem(n) for n in ("adj_free", "ego_init", "slot_rdy", "agg_done", "agg_out", "turned", "updated", "ln_var", "ln_root",
                             "dve_chain2"))
        block = ctx.enter_context(nc.Block())
        SEG = [(512 * b, min(512, SPAD - 512 * b)) for b in range(-(-SPAD // 512))]
        TB = 5

        @block.sync
        def _(sp):
            with sp.Fori(0, ROUNDS * NT // UK) as i:
                for k in range(UK):
                    rows = [(sp.snap(((i * UK + k) % NT) * NP + p0), p0, p1) for p0, p1 in ((0, 112), (112, NP))]
                    sp.wait_ge(s_afree, i * UK + k + 1)
                    for row, p0, p1 in rows:
                        sp.dma_start(at[k][p0:p1, :], m.adj[bass.ds(row, p1 - p0), :]).then_inc(s_at[k], 16)

        @block.vector
        def _(v):
            link = Chain(v, s_dv)
            link(nc.vector.tensor_copy(ego[:, :, :], m.x[:, :, :]))
            link(nc.vector.tensor_copy(acc[:, :, :], m.x[:, :, :]))
            with v.Fori(0, ROUNDS) as r:
                with v.Fori(0, NT // UK) as i:
                    for k in range(UK):
                        n = r * NT + i * UK + k
                        v.wait_ge(s_afree, n + 1)
                        nc.vector.tensor_copy(slot[k][:, :], ego[:, bass.ds(i * UK + k, 1), :].rearrange("p a d -> p (a d)"))\
                            .then_inc(s_slot, 1)
                for b in range(NT // TB):
                    v.wait_ge(s_tr, r * (NT // TB) + b + 1)
                    e = ego[:, b * TB:(b + 1) * TB, :]
                    g = pa[b][0:NP, 0:TB * D].rearrange("p (k d) -> p k d", d=D)
                    nc.vector.scalar_tensor_tensor(out=e, in0=e, scalar=1.0, in1=g, op0=ALU.add, op1=ALU.mult)\
                        .then_inc(s_upd, 1)
                v.wait_ge(s_upd, (r * 2 + 1) * (NT // TB))
                for b in range(NT // TB):
                    e, a = (t[:, b * TB:(b + 1) * TB, :] for t in (ego, acc))
                    nc.vector.tensor_tensor(a, a, e, ALU.add).then_inc(s_upd, 1)
                v.wait_ge(s_upd, (r + 1) * 2 * (NT // TB))
            link(nc.vector.scalar_tensor_tensor(out=acc[:, :, :], in0=acc[:, :, :], scalar=1.0 / (ROUNDS + 1),
                                                in1=m.x[:, :, :], op0=ALU.mult, op1=ALU.add))
            layer_norm(nc, link, acc[:, :, :], tmp[:, :, :], stats, m.x[:, :, :], m.eps, s_ln, s_rt, v)

        @block.scalar
        def _(act):
            with act.Fori(0, ROUNDS) as r:
                act.wait_ge(s_agg, r + 1)
                for b, (c0, w) in enumerate(SEG):
                    nc.scalar.copy(agg_t[:, c0:c0 + w], pa[b][0:D, 0:w]).then_inc(s_out, 1)
            act.wait_ge(s_ln, 1)
            nc.scalar.activation(stats[:, 1, :], stats[:, 1, :], ACT.Sqrt, bias=m.eps[:, :]).then_inc(s_rt, 1)

        @block.tensor
        def _(pe):
            pe.sem_inc(s_afree, UK)

            def product(r, t, k, first, last):
                n = r * NT + t
                pe.wait_ge(s_slot, n + 1)
                pe.wait_ge(s_at[k], (r * (NT // UK) + (t - k) // UK + 1) * 32)
                for b, (c0, w) in enumerate(SEG):
                    mm = nc.tensor.matmul(pa[b][0:D, 0:w], slot[k][:, :], at[k][:, c0:c0 + w], start=first, stop=last)
                mm.then_inc(s_afree, 1)

            with pe.Fori(0, ROUNDS) as r:
                for k in range(UK):
                    product(r, k, k, k == 0, False)
                with pe.Fori(1, NT // UK - 1) as i:
                    for k in range(UK):
                        n = r * NT + i * UK + k
                        pe.wait_ge(s_slot, n + 1)
                        pe.wait_ge(s_at[k], (r * (NT // UK) + i + 1) * 32)
                        for b, (c0, w) in enumerate(SEG):
                            mm = nc.tensor.matmul(pa[b][0:D, 0:w], slot[k][:, :], at[k][:, c0:c0 + w], start=False, stop=False)
                        mm.then_inc(s_afree, 1)
                for k in range(UK):
                    product(r, NT - UK + k, k, False, k == UK - 1)
                pe.wait_ge(s_afree, (r + 1) * NT + UK)
                pe.sem_inc(s_agg, 1)
                pe.wait_ge(s_out, (r + 1) * len(SEG))
                for b in range(NT // TB):
                    for j in range(TB):
                        t = b * TB + j
                        mm = nc.tensor.transpose(pa[b][0:NP, j * D:(j + 1) * D], agg_t[:, t * NP:(t + 1) * NP],
                                                 m.ident[0:D, 0:D])
                    mm.then_inc(s_tr, 1)
                pe.wait_ge(s_upd, (r * 2 + 1) * (NT // TB))


def phase_conv(nc, m, layer, x_in, w_msg, w_edge, w_root, bias, conv_out, final):
    with ExitStack() as ctx:
        def sb(name, shape, dt=F32):
            return ctx.enter_context(nc.sbuf_tensor(f"{name}_{layer}", shape, dt))

        def sem(name):
            return ctx.enter_context(nc.semaphore(f"{name}_{layer}"))

        U = 2
        MC = 4
        wmr = sb("wmr", [D, 2 * D])
        we = sb("we", [P, 4, D])
        bb = sb("bb", [NP, D])
        xt = sb("xt", [D, N])
        y_sb = sb("y_sb", [NP, NT, D])
        z = sb("z", [NP, NT, D])
        agg = sb("agg", [NP, NT, D])
        tmp = sb("tmp", [NP, NT, D])
        stats = sb("stats", [NP, 2, NT])
        gi = [sb(f"gi{k}", [P, 4], I32) for k in range(U)]
        got = [sb(f"got{k}", [P, 4, D]) for k in range(U)]
        ea = [sb(f"ea{k}", [P, 4 * DE]) for k in range(U)]
        eat = [sb(f"eat{k}", [P, P]) for k in range(U)]
        mk = [sb(f"mk{k}", [D, CH], BF16) for k in range(U)]
        sc = [sb(f"sc{k}", [D, CH]) for k in range(U)]
        so = [sb(f"so{k}", [P, 4, D]) for k in range(U)]
        ps_m = [ctx.enter_context(nc.psum_tensor(f"ps_m{k}_{layer}", [P, 512], F32)) for k in range(U)]
        ps_e = [ctx.enter_context(nc.psum_tensor(f"ps_e{k}_{layer}", [P, 512], F32)) for k in range(U)]
        ps_o = [ctx.enter_context(nc.psum_tensor(f"ps_o{k}_{layer}", [P, 512], F32)) for k in range(U)]
        s_wl, s_wz, s_t, s_te, s_y, s_ye, s_ys = (sem(n) for n in ("w_in", "w_zero", "xt_up", "xt_out", "y_up", "y_out", "y_stored"))
        s_gi, s_gidle = sem("idx_rdy"), sem("rows_free")
        s_got = [sem(f"rows_in{k}") for k in range(U)]
        s_ea, s_mk = [sem(f"ea_in{k}") for k in range(U)], [sem(f"mask_in{k}") for k in range(U)]
        s_ef, s_mf = sem("ea_free"), sem("mask_free")
        s_et, s_eat, s_msg, s_scan, s_st, s_so = (sem(n) for n in ("ea_up", "eat_rdy", "msg_done", "scanned", "seg_up", "seg_rdy"))
        s_sw = [sem(f"seg_stored{k}") for k in range(U)]
        s_end, s_agg, s_dv, s_ln, s_rt, s_res = (sem(n) for n in ("agg_ready", "agg_in", "chain", "var", "root", "result"))
        HC = NC // U
        mask_c = m.mask.rearrange("p e -> (p e)")
        ea_full = m.ea
        tile_w = 2 * D

        block = ctx.enter_context(nc.Block())

        @block.sync
        def _(sp):
            sp.dma_start(wmr[:, 0:D], w_msg).then_inc(s_wl, 16)
            sp.dma_start(wmr[:, D:2 * D], w_root).then_inc(s_wl, 16)
            sp.dma_start(bb[:, :], bias.unsqueeze(0).to_broadcast([NP, D])).then_inc(s_wl, 16)
            sp.wait_ge(s_wz, 1)
            for j in range(4):
                sp.dma_start(we[j * DE:(j + 1) * DE, j, :], w_edge).then_inc(s_wl, 16)

            with sp.Fori(0, HC - 1) as i:
                for k in range(U):
                    c = i * U + k
                    edge = sp.snap(c * CH)
                    sp.wait_ge(s_ef, c + 1)
                    sp.dma_start(ea[k][:, :], ea_full[bass.ds(edge, CH), :].rearrange("(p j) f -> p (j f)", j=4))\
                        .then_inc(s_ea[k], 16)
                    sp.wait_ge(s_mf, c + 1)
                    sp.nop(nofuse=True)
                    sp.dma_start(mk[k][:, :], mask_c[bass.ds(edge, CH)].unsqueeze(0).to_broadcast([D, CH]))\
                        .then_inc(s_mk[k], 16)
            for k in range(U):
                c = NC - U + k
                sp.wait_ge(s_ef, c + 1)
                if c < NC - 1:
                    sp.dma_start(ea[k][:, :], ea_full[c * CH:(c + 1) * CH, :].rearrange("(p j) f -> p (j f)", j=4))\
                        .then_inc(s_ea[k], 16)
                else:
                    n = E - c * CH
                    sp.dma_start(ea[k][0:n // 4, :], ea_full[c * CH:c * CH + n // 4 * 4, :].rearrange("(p j) f -> p (j f)", j=4))\
                        .then_inc(s_ea[k], 16)
                    sp.dma_start(ea[k][n // 4:n // 4 + 1, 0:n % 4 * DE],
                                 ea_full[c * CH + n // 4 * 4:E, :].rearrange("(o j) f -> o (j f)", o=1)).then_inc(s_ea[k], 16)
                sp.wait_ge(s_mf, c + 1)
                sp.dma_start(mk[k][:, :], mask_c[c * CH:(c + 1) * CH].unsqueeze(0).to_broadcast([D, CH])).then_inc(s_mk[k], 16)

        @block.gpsimd
        def _(g):
            nc.gpsimd.memset(we[:, :, :], 0.0).then_inc(s_wz, 1)
            g.wait_ge(s_ys, 16)
            with g.Fori(0, HC) as i:
                for k in range(U):
                    c = i * U + k
                    g.wait_ge(s_gi, c + 1)
                    g.nop(nofuse=True)
                    for j in range(4):
                        g.indirect_dma_start(got[k][:, j, :], None, m.y,
                                             bass.IndirectOffsetOnAxis(ap=gi[k][:, j:j + 1], axis=0)).then_inc(s_got[k], 16)
            g.wait_ge(s_end, 1)
            for t in range(NT):
                g.indirect_dma_start(agg[:, t, :], None, m.seg,
                                     bass.IndirectOffsetOnAxis(ap=m.end_idx[:, t:t + 1], axis=0)).then_inc(s_agg, 16)
            g.wait_ge(s_agg, 16 * NT)

        @block.vector
        def _(v):
            link = Chain(v, s_dv)
            v.wait_ge(s_wl, 16 * 7)
            for t in range(NT):
                v.wait_ge(s_y, t + 1)
                bank = ps_o[t % 2]
                nc.vector.tensor_copy(y_sb[:, t, :], bank[0:NP, 0:D])
                nc.vector.tensor_tensor(z[:, t, :], bank[0:NP, D:2 * D], bb[:, :], ALU.add).then_inc(s_ye, 1)
            nc.vector.memset(sc[U - 1][:, CH - 1:CH], 0.0).then_inc(s_scan, 1)

            with v.Fori(0, HC) as i:
                for k in range(U):
                    c = i * U + k
                    v.wait_ge(s_gidle, c + 1)
                    nc.vector.tensor_copy(gi[k][:, :], m.src_idx[:, bass.ds(c * 4, 4)]).then_inc(s_gi, 1)
                for k in range(U):
                    c = i * U + k
                    v.wait_ge(s_msg, c + 1)
                    v.wait_ge(s_mk[k], (i + 1) * 16)
                    v.wait_ge(s_scan, c + 1)
                    v.wait_ge(s_st, c + 1)
                    nc.vector.tensor_tensor_scan(sc[k][:, :], mk[k][:, :], ps_m[k][0:D, :], sc[k - 1][:, CH - 1:CH],
                                                 ALU.add, ALU.max).then_inc(s_scan, 1)
            v.wait_ge(s_agg, 16 * NT)
            link(nc.vector.tensor_tensor(z[:, :, :], z[:, :, :], agg[:, :, :], ALU.add))
            res = tmp if final else conv_out
            link(nc.vector.scalar_tensor_tensor(out=res[:, :, :], in0=z[:, :, :], scalar=SLOPE, in1=z[:, :, :],
                                                op0=ALU.mult, op1=ALU.max))
            if final:
                link(nc.vector.tensor_tensor(z[:, :, :], tmp[:, :, :], m.x[:, :, :], ALU.add))
                layer_norm(nc, link, z[:, :, :], tmp[:, :, :], stats, agg[:, :, :], m.eps, s_ln, s_rt, v)
                v.sem_inc(s_res, 1)

        @block.scalar
        def _(act):
            for t in range(NT):
                act.wait_ge(s_t, t + 1)
                nc.scalar.copy(xt[:, t * NP:(t + 1) * NP], ps_m[t % 2][0:D, 0:NP]).then_inc(s_te, 1)
            act.wait_ge(s_ye, NT)
            act.dma_start(m.y.rearrange("(k p) d -> p k d", p=NP), y_sb[:, :, :]).then_inc(s_ys, 16)
            act.wait_ge(s_ys, 16)

            def chunk_out(c, k):
                act.wait_ge(s_et, c + 1)
                nc.scalar.copy(eat[k][:, :], ps_e[k][:, 0:P]).then_inc(s_eat, 1)

            def maxima_out(c, k, wait_store):
                act.wait_ge(s_st, c + 1 + U)
                if wait_store is not None:
                    act.wait_ge(s_sw[k], wait_store)
                nc.scalar.copy(so[k][:, :, :], ps_o[k][:, 0:4 * D].rearrange("p (j d) -> p j d", d=D)).then_inc(s_so, 1)
                edge = c * CH if isinstance(c, int) else act.snap(c * CH)
                act.wait_ge(s_so, c + 1)
                rows = m.seg[bass.ds(edge, CH), :]
                act.dma_start(rows.rearrange("(p j) d -> p (j d)", j=4), so[k][:, :, :].rearrange("p j d -> p (j d)"))\
                    .then_inc(s_sw[k], 16)

            chunk_out(0, 0)
            chunk_out(1, 1)
            for k in range(U):
                maxima_out(k, k, None)
                chunk_out(U + k, k)
            with act.Fori(1, HC - 1) as i:
                for k in range(U):
                    maxima_out(i * U + k, k, i * 16)
                    chunk_out(i * U + k + U, k)
            for k in range(U):
                maxima_out(NC - U + k, k, (HC - 1) * 16)
            for k in range(U):
                act.wait_ge(s_sw[k], HC * 16)
            act.sem_inc(s_end, 1)
            if final:
                act.wait_ge(s_ln, 1)
                nc.scalar.activation(stats[:, 1, :], stats[:, 1, :], ACT.Sqrt, bias=m.eps[:, :]).then_inc(s_rt, 1)
                act.wait_ge(s_res, 1)
                act.dma_start(m.out.rearrange("(k p) d -> p k d", p=NP), agg[:, :, :]).then_inc(s_ys, 16)
                act.wait_ge(s_ys, 32)

        @block.tensor
        def _(pe):
            pe.sem_inc(s_gidle, U)
            pe.sem_inc(s_ef, U)
            pe.sem_inc(s_mf, U)
            pe.sem_inc(s_st, U)
            for t in range(NT):
                if t >= 2:
                    pe.wait_ge(s_te, t - 1)
                nc.tensor.transpose(ps_m[t % 2][0:D, 0:NP], x_in[:, t, :], m.ident[0:NP, 0:NP]).then_inc(s_t, 1)
            pe.wait_ge(s_te, NT)
            pe.wait_ge(s_wl, 16 * 7)
            for t in range(NT):
                if t >= 2:
                    pe.wait_ge(s_ye, t - 1)
                nc.tensor.matmul(ps_o[t % 2][0:NP, 0:tile_w], xt[:, t * NP:(t + 1) * NP], wmr[:, :],
                                 start=True, stop=True).then_inc(s_y, 1)
            pe.wait_ge(s_ye, NT)

            def turn_ea(c, k, arrived):
                pe.wait_ge(s_ea[k], arrived)
                nc.tensor.transpose(ps_e[k][:, 0:P], ea[k][:, :], m.ident[:, :]).then_inc(s_et, 1)
                pe.wait_ge(s_et, c + 1)
                pe.sem_inc(s_ef, 1)

            def messages(c, k, arrived):
                pe.wait_ge(s_eat, c + 1)
                pe.wait_ge(s_got[k], arrived)
                if not isinstance(c, int) or c >= U:
                    pe.wait_ge(s_scan, c)
                cols = ps_m[k][0:D, :].rearrange("d (p j) -> d j p", j=4)
                for j in range(4):
                    nc.tensor.matmul(cols[:, j, :], we[:, j, :], eat[k][:, :], start=j == 0, stop=False,
                                     skip_group_check=True)
                for j in range(4):
                    mm = nc.tensor.matmul(cols[:, j, :], got[k][:, j, :], m.ident[:, :], start=False, stop=j == 3,
                                          skip_group_check=True)
                mm.then_inc(s_msg, 1)
                pe.wait_ge(s_msg, c + 1)
                pe.sem_inc(s_gidle, 1)

            def turn_maxima(c, k):
                pe.wait_ge(s_scan, c + 2)
                if not isinstance(c, int) or c >= U:
                    pe.wait_ge(s_so, c + 1 - U)
                pe.sem_inc(s_mf, 1)
                cols = sc[k][:, :].rearrange("d (p j) -> d j p", j=4)
                for j in range(4):
                    mm = nc.tensor.transpose(ps_o[k][:, j * D:(j + 1) * D], cols[:, j, :], m.ident[0:D, 0:D])
                mm.then_inc(s_st, 1)

            turn_ea(0, 0, 16)
            turn_ea(1, 1, 16)
            messages(0, 0, 64)
            messages(1, 1, 64)
            for k in range(U):
                turn_ea(U + k, k, 32)
                turn_maxima(k, k)
                messages(U + k, k, 128)
            with pe.Fori(1, HC - 2) as i:
                for k in range(U):
                    c = i * U + k
                    turn_ea(c + U, k, (i + 2) * 16)
                    turn_maxima(c, k)
                    messages(c + U, k, (i + 2) * 64)
            for k in range(U):
                c = NC - 2 * U + k
                turn_ea(c + U, k, HC * 16 + (16 if c + U == NC - 1 else 0))
                turn_maxima(c, k)
                messages(c + U, k, HC * 64)
            for k in range(U):
                turn_maxima(NC - U + k, k)


def gnn_program(nc, x, src, dst, edge_attr, edge_weight, weights, out):
    with ExitStack() as ctx:
        m = Mem()
        m.x_in, m.src, m.dst, m.ea, m.w, m.out = x, src, dst, edge_attr, edge_weight, out
        persistent(nc, ctx, m)
        phase_prepare(nc, m)
        phase_adjacency(nc, m)
        phase_propagate(nc, m)
        c1 = ctx.enter_context(nc.sbuf_tensor("c1", [NP, NT, D], F32))
        phase_conv(nc, m, 1, m.x, *weights[0:4], c1, False)
        phase_conv(nc, m, 2, c1, *weights[4:8], None, True)


_INS = ["x", "src", "dst", "edge_attr_32", "edge_weight",
        "L1_gnn_W1_msg", "L1_gnn_W1_edge", "L1_gnn_W1_root", "L1_gnn_b1",
        "L1_gnn_W2_msg", "L1_gnn_W2_edge", "L1_gnn_W2_root", "L1_gnn_b2"]


def kernel(**inputs):
    import numpy as np
    import concourse.bacc as bacc
    from concourse.bass_utils import run_bass_kernel_spmd as run

    nc = bacc.Bacc("TRN2", target_bir_lowering=False, num_devices=1)
    arrays, args = {}, []
    for name in _INS:
        a = np.ascontiguousarray(inputs[name])
        arrays[f"in_{name}"] = a
        args.append(nc.dram_tensor(f"in_{name}", a.shape, mybir.dt.from_np(a.dtype), kind="ExternalInput").ap())
    out = nc.dram_tensor("out_x", (N, D), F32, kind="ExternalOutput").ap()
    gnn_program(nc, *args[:5], args[5:], out)
    return run(nc, [arrays], core_ids=[0]).results[0]["out_x"]
```

```python
from contextlib import ExitStack

import concourse.bass as bass
from concourse import mybir

F32, BF16, I32 = mybir.dt.float32, mybir.dt.bfloat16, mybir.dt.int32
ALU, ACT, AX = mybir.AluOpType, mybir.ActivationFunctionType, mybir.AxisListType

P = 128
N, D, E, DE = 3125, 96, 103125, 32
ROUNDS = 3
EPS = 1e-5
SLOPE = 0.01

NB = 128
NA = -(-N // NB)
SPAD = NA * NB
NP = 125
NT = N // NP
G = NP // NA
NG = N // G
GT = NG // NP
GK = NP // G

CH = 512
NC = -(-E // CH)
ROW = 32
EW = 26 * ROW
EP = P * EW
PROWS = EP // ROW
WR = 8
WIN = WR * ROW
HALF = WIN // P
STEPS = GK * HALF
DPAD = N
SKIP = float(1 << 24)
FAR = -3.3e38


def full_rows(width):
    return E // width, E % width


class Chain:

    def __init__(self, eng, sem):
        self.eng, self.sem, self.n = eng, sem, 0

    def __call__(self, ins):
        self.n += 1
        ins.then_inc(self.sem, 1)
        self.eng.wait_ge(self.sem, self.n)


class Mem:
    pass


def persistent(nc, ctx, m):
    def sb(name, shape, dt=F32):
        return ctx.enter_context(nc.sbuf_tensor(name, shape, dt))

    m.ident = sb("ident", [P, P])
    m.iota = sb("iota", [P, P])
    m.src_idx = sb("src_idx", [P, EP // P], I32)
    m.x = sb("x_nat", [NP, NT, D])
    m.end_idx = sb("end_idx", [NP, NT], I32)
    m.zero = sb("zero_row", [NP, D])
    m.ones = sb("ones", [P, 1])
    m.ramp = sb("ramp", [P, P], I32)
    m.unsorted = sb("unsorted", [1, 1], I32)
    m.crowded = sb("crowded", [1, 1], I32)
    m.dst_sb = sb("dst_sb", [P, EW], I32)
    m.src_sb = sb("src_sb", [P, EW], I32)
    m.w_sb = sb("w_sb", [P, EW])
    m.before = sb("before", [P, 1], I32)
    m.eps = sb("eps", [NP, 1])

    def dram(name, shape, dt=F32):
        return nc.dram_tensor(name, shape, dt, kind="Internal").ap()

    m.packed = dram("packed", (PROWS, 3 * ROW))
    m.mask = dram("mask", (P, EW), BF16)
    m.ends = dram("ends", (1 + SPAD,), I32)
    m.adj = dram("adj", (N, SPAD))
    m.src_s = dram("src_sorted", (EP,), I32)
    m.dst_s = dram("dst_sorted", (EP,), I32)
    m.w_s = dram("w_sorted", (EP,))
    m.ea_s = dram("ea_sorted", (EP, DE))
    m.place = dram("place", (SPAD,), I32)
    m.y = dram("y_rows", (N, D))
    m.seg = dram("seg", (NC * CH + 1, D))


def load_source_order(nc, m, eng, sem, src, padded):
    idx = m.src_idx[:, :].rearrange("p (c j) -> p c j", j=4)
    if padded:
        eng.dma_start(idx, src.rearrange("(c p j) -> p c j", p=P, j=4)).then_inc(sem, 16)
        return 16
    full, rest = full_rows(CH)
    eng.dma_start(idx[:, 0:full, :], src[0:full * CH].rearrange("(c p j) -> p c j", p=P, j=4)).then_inc(sem, 16)
    eng.dma_start(idx[0:rest // 4, full, :],
                  src[full * CH:E - rest % 4].rearrange("(p j) -> p j", j=4)).then_inc(sem, 16)
    eng.dma_start(idx[rest // 4:rest // 4 + 1, full, 0:rest % 4], src[E - rest % 4:E].unsqueeze(0)).then_inc(sem, 16)
    return 48


def phase_count(nc, m):
    with ExitStack() as ctx:
        def sb(name, shape, dt=F32):
            return ctx.enter_context(nc.sbuf_tensor(name, shape, dt))

        def sem(name):
            return ctx.enter_context(nc.semaphore(name))

        part = sb("part", [P, EW], I32)
        drop = sb("drop", [P, EW])
        drops = sb("drops", [P, 1])
        da = sb("da", [P, EW])
        db = sb("db", [P, EW])
        HT = 8
        oh_a = [sb(f"oh_a{k}", [P, HT, NA], BF16) for k in range(2)]
        oh_b = [sb(f"oh_b{k}", [P, HT, NB], BF16) for k in range(2)]
        cnt = sb("cnt", [NA, NB])
        run = sb("run", [NA, NB])
        zeros = sb("zeros", [NA, NB])
        ends_i = sb("ends_i", [NA, NB], I32)
        tri = sb("tri", [NA, NA])
        first = sb("first", [1, 1], I32)
        hist = ctx.enter_context(nc.psum_tensor("hist", [NA, NB], F32))
        carry = ctx.enter_context(nc.psum_tensor("carry", [NA, 1], F32))
        bad = ctx.enter_context(nc.psum_tensor("bad", [1, 1], F32))

        s_const, s_ramp, s_fill, s_load, s_vec = (sem(n) for n in ("const", "ramp_rdy", "filled", "loaded", "vec"))
        s_oh, s_ohfree, s_drop, s_bad = sem("onehots_rdy"), sem("onehots_free"), sem("drops_rdy"), sem("bad_rdy")
        s_tot, s_carry, s_ends, s_out = sem("totals_rdy"), sem("carry_rdy"), sem("ends_rdy"), sem("stored")
        s_gz, s_order, s_ea = sem("pool_chain"), sem("ordered_in"), sem("ea_copied")
        block = ctx.enter_context(nc.Block())
        full, rest = full_rows(EW)
        LOADS = 9

        @block.sync
        def _(sp):
            sp.wait_ge(s_fill, 5)
            for buf, arr in ((m.dst_sb, m.dst), (m.src_sb, m.src), (m.w_sb, m.w)):
                sp.dma_start(buf[0:full, :], arr[0:full * EW].rearrange("(p e) -> p e", e=EW)).then_inc(s_load, 16)
                sp.dma_start(buf[full:full + 1, 0:rest], arr[full * EW:E].unsqueeze(0)).then_inc(s_load, 16)
            with nc.allow_non_contiguous_dma(reason="one neighbour per partition"):
                sp.dma_start(m.before[1:full + 1, :],
                             m.dst[0:full * EW].rearrange("(p e) -> p e", e=EW)[:, EW - 1:EW]).then_inc(s_load, 16)
            sp.dma_start(m.x[:, :, :], m.x_in.rearrange("(k p) d -> p k d", p=NP)).then_inc(s_load, 16)
            sp.dma_start(m.seg[NC * CH:NC * CH + 1, :], m.zero[0:1, :]).then_inc(s_load, 16)
            sp.wait_ge(s_ends, 1)
            sp.dma_start(m.ends[1:1 + SPAD].rearrange("(a b) -> a b", b=NB), ends_i[:, :]).then_inc(s_out, 16)
            sp.dma_start(m.ends[0:1].unsqueeze(0), first[:, :]).then_inc(s_out, 16)
            sp.wait_ge(s_out, 32)
            sp.wait_ge(s_load, 16 * LOADS)

        @block.gpsimd
        def _(g):
            nc.gpsimd.memset(m.src_idx[:, :], 0).then_inc(s_fill, 1)
            nc.gpsimd.iota(m.ramp[:, :], pattern=[[1, P]], base=0, channel_multiplier=0).then_inc(s_ramp, 1)
            nc.gpsimd.memset(m.ident[:, :], 0.0).then_inc(s_gz, 1)
            nc.gpsimd.memset(tri[:, :], 1.0).then_inc(s_gz, 1)
            g.wait_ge(s_gz, 2)
            nc.gpsimd.affine_select(out=m.ident[:, :], in_=m.ident[:, :], compare_op=ALU.not_equal, fill=1.0, base=0,
                                    pattern=[[-1, P]], channel_multiplier=1).then_inc(s_const, 1)
            nc.gpsimd.affine_select(out=tri[:, :], in_=tri[:, :], compare_op=ALU.is_gt, fill=0.0, base=0,
                                    pattern=[[1, NA]], channel_multiplier=-1).then_inc(s_const, 1)

        @block.scalar
        def _(act):
            act.wait_ge(s_fill, 5)
            n = load_source_order(nc, m, act, s_order, m.src, False)
            act.dma_start(m.ea_s[0:E, :].rearrange("(p e) f -> p (e f)", p=NP), m.ea.rearrange("(p e) f -> p (e f)", p=NP))\
                .then_inc(s_ea, 16)
            act.wait_ge(s_order, n)
            act.wait_ge(s_ea, 16)

        @block.vector
        def _(v):
            link = Chain(v, s_vec)
            nc.vector.memset(m.dst_sb[:, :], DPAD).then_inc(s_fill, 1)
            nc.vector.memset(m.src_sb[:, :], 0).then_inc(s_fill, 1)
            nc.vector.memset(m.w_sb[:, :], 0.0).then_inc(s_fill, 1)
            for buf, value in ((m.zero, 0.0), (m.eps, EPS), (m.ones, 1.0), (first, 0), (zeros, 0.0)):
                nc.vector.memset(buf[:, :], value)
            nc.vector.memset(m.before[:, :], -1).then_inc(s_fill, 1)
            v.wait_ge(s_ramp, 1)
            link(nc.vector.tensor_copy(m.iota[:, :], m.ramp[:, :]))
            v.wait_ge(s_load, 16 * LOADS)
            dst = m.dst_sb
            link(nc.vector.tensor_tensor(drop[:, 1:EW], dst[:, 1:EW], dst[:, 0:EW - 1], ALU.is_lt))
            link(nc.vector.tensor_tensor(drop[:, 0:1], dst[:, 0:1], m.before[:, :], ALU.is_lt))
            nc.vector.tensor_reduce(drops[:, :], drop[:, :], AX.X, ALU.max).then_inc(s_drop, 1)
            link(nc.vector.tensor_scalar(part[:, :], dst[:, :], 7, None, ALU.arith_shift_right))
            link(nc.vector.tensor_copy(da[:, :], part[:, :]))
            link(nc.vector.tensor_scalar(part[:, :], dst[:, :], NB - 1, None, ALU.bitwise_and))
            link(nc.vector.tensor_copy(db[:, :], part[:, :]))
            with v.Fori(0, EW // HT // 2) as i:
                for k in range(2):
                    v.wait_ge(s_ohfree, i * 2 + k + 1)
                    cols = bass.ds((i * 2 + k) * HT, HT)
                    nc.vector.tensor_tensor(oh_a[k][:, :, :], m.iota[:, 0:NA].unsqueeze(1).to_broadcast([P, HT, NA]),
                                            da[:, cols].unsqueeze(2).to_broadcast([P, HT, NA]),
                                            ALU.is_equal).then_inc(s_oh, 1)
                    nc.vector.tensor_tensor(oh_b[k][:, :, :], m.iota[:, :].unsqueeze(1).to_broadcast([P, HT, NB]),
                                            db[:, cols].unsqueeze(2).to_broadcast([P, HT, NB]),
                                            ALU.is_equal).then_inc(s_oh, 1)
            v.wait_ge(s_ohfree, EW // HT + 2)
            link(nc.vector.tensor_copy(cnt[:, :], hist[:, :]))
            nc.vector.tensor_tensor_scan(run[:, :], cnt[:, :], zeros[:, :], 0.0, ALU.add, ALU.add).then_inc(s_tot, 1)
            v.wait_ge(s_carry, 1)
            nc.vector.tensor_scalar(ends_i[:, :], run[:, :], carry[:, 0:1], None, ALU.add).then_inc(s_ends, 1)
            v.wait_ge(s_bad, 1)
            link(nc.vector.tensor_copy(m.unsorted[:, :], bad[:, :]))

        @block.tensor
        def _(pe):
            pe.sem_inc(s_ohfree, 2)
            n_slots = EW // HT

            def count(k, slot, first, last):
                pe.wait_ge(s_oh, (slot + 1) * 2)
                for t in range(HT):
                    mm = nc.tensor.matmul(hist[:, :], oh_a[k][:, t, :], oh_b[k][:, t, :],
                                          start=first and t == 0, stop=last and t == HT - 1)
                mm.then_inc(s_ohfree, 1)

            count(0, 0, True, False)
            count(1, 1, False, False)
            with pe.Fori(1, n_slots // 2 - 1) as i:
                for k in range(2):
                    count(k, i * 2 + k, False, False)
            count(0, n_slots - 2, False, False)
            count(1, n_slots - 1, False, True)
            pe.wait_ge(s_drop, 1)
            nc.tensor.matmul(bad[:, :], drops[:, :], m.ones[:, :], start=True, stop=True).then_inc(s_bad, 1)
            pe.wait_ge(s_tot, 1)
            pe.wait_ge(s_const, 2)
            nc.tensor.matmul(carry[:, :], tri[:, :], run[:, NB - 1:NB], start=True, stop=True).then_inc(s_carry, 1)


def phase_sort(nc, m):
    with ExitStack() as ctx:
        def sb(name, shape, dt=F32):
            return ctx.enter_context(nc.sbuf_tensor(name, shape, dt))

        def sem(name):
            return ctx.enter_context(nc.semaphore(name))

        lower = sb("lower", [P, P])
        wide = sb("wide", [P, P])
        same = sb("same", [P, P])
        sameb = sb("sameb", [P, P])
        key = sb("key", [P, 1], I32)
        one_src = sb("one_src", [P, 1], I32)
        one_w = sb("one_w", [P, 1])
        one_ea = sb("one_ea", [P, DE])
        base = sb("base", [P, 1], I32)
        prior = sb("prior", [P, 1])
        total = sb("total", [P, 1])
        skip = sb("skip", [P, 1])
        rank = sb("rank", [P, 1], I32)
        nxt = sb("nxt", [P, 1], I32)
        nkey = sb("nkey", [P, 1], I32)
        across = ctx.enter_context(nc.psum_tensor("across", [P, P], F32))
        s_low, s_init, s_go, s_key, s_wide, s_acr, s_base, s_calc, s_rank, s_put, s_ea, s_re = (
            sem(n) for n in ("lower_rdy", "place_set", "batch_go", "key_rdy", "wide_rdy", "across_rdy", "base_in", "calc",
                             "rank_rdy", "put", "ea_in", "reloaded"))
        s_low0 = sem("lower_set")
        block = ctx.enter_context(nc.Block())
        full, rest = full_rows(EW)
        PUTS = 5

        def columns(eng, body):
            with eng.Fori(0, rest) as t:
                body(t, True)
            with eng.Fori(rest, EW) as t:
                body(t, False)

        @block.sync
        def _(sp):
            with sp.If(sp.value_load(m.unsorted[0:1, 0:1]) != 0):
                sp.dma_start(m.place.rearrange("(a b) -> a b", b=NB), m.ends[0:SPAD].rearrange("(a b) -> a b", b=NB))\
                    .then_inc(s_init, 16)
                ea_cols = m.ea[0:full * EW, :].rearrange("(p t) f -> t p f", t=EW)

                def features(t, more):
                    sp.wait_ge(s_go, t + 1)
                    sp.nop(nofuse=True)
                    sp.dma_start(one_ea[0:full, :], ea_cols[bass.ds(t, 1), :, :].rearrange("o p f -> (o p) f"))\
                        .then_inc(s_ea, 16)
                    if more:
                        sp.dma_start(one_ea[full:full + 1, :], m.ea[bass.ds(t + full * EW, 1), :]).then_inc(s_ea, 16)

                columns(sp, features)
                sp.wait_ge(s_go, EW + 1)
                for buf, arr in ((m.dst_sb, m.dst_s), (m.src_sb, m.src_s), (m.w_sb, m.w_s)):
                    sp.dma_start(buf[:, :], arr.rearrange("(p e) -> p e", e=EW)).then_inc(s_re, 16)
                with nc.allow_non_contiguous_dma(reason="one neighbour per partition"):
                    sp.dma_start(m.before[1:P, :],
                                 m.dst_s[0:EP - EW].rearrange("(p e) -> p e", e=EW)[:, EW - 1:EW]).then_inc(s_re, 16)
                n = load_source_order(nc, m, sp, s_re, m.src_s, True)
                sp.wait_ge(s_re, 64 + n)

        @block.gpsimd
        def _(g):
            with g.If(g.value_load(m.unsorted[0:1, 0:1]) != 0):
                nc.gpsimd.memset(lower[:, :], 1.0).then_inc(s_low0, 1)
                nc.gpsimd.memset(one_ea[:, :], 0.0).then_inc(s_low0, 1)
                g.wait_ge(s_low0, 2)
                nc.gpsimd.affine_select(out=lower[:, :], in_=lower[:, :], compare_op=ALU.is_gt, fill=0.0, base=0,
                                        pattern=[[-1, P]], channel_multiplier=1).then_inc(s_low, 1)
                g.wait_ge(s_init, 16)
                g.wait_ge(s_low, 1)
                g.sem_inc(s_go, 1)

                def put(t, more):
                    g.wait_ge(s_key, t + 1)
                    g.nop(nofuse=True)
                    g.indirect_dma_start(base[:, :], None, m.place.unsqueeze(1),
                                         bass.IndirectOffsetOnAxis(ap=key[:, :], axis=0)).then_inc(s_base, 16)
                    g.wait_ge(s_ea, (t + 1) * 32 if more else t * 16 + (rest + 1) * 16)
                    g.nop(nofuse=True)
                    g.wait_ge(s_rank, t + 1)
                    g.nop(nofuse=True)
                    for table, buf in ((m.src_s.unsqueeze(1), one_src), (m.dst_s.unsqueeze(1), key),
                                       (m.w_s.unsqueeze(1), one_w), (m.ea_s, one_ea)):
                        g.indirect_dma_start(table, bass.IndirectOffsetOnAxis(ap=rank[:, :], axis=0), buf[:, :], None)\
                            .then_inc(s_put, 16)
                    g.indirect_dma_start(m.place.unsqueeze(1), bass.IndirectOffsetOnAxis(ap=nkey[:, :], axis=0), nxt[:, :],
                                         None, bounds_check=SPAD - 1, oob_is_err=False).then_inc(s_put, 16)
                    g.wait_ge(s_put, (t + 1) * 16 * PUTS)
                    g.nop(nofuse=True)
                    g.sem_inc(s_go, 1)

                columns(g, put)

        @block.vector
        def _(v):
            with v.If(v.value_load(m.unsorted[0:1, 0:1]) != 0):
                STEPS_V = 7

                def rank_batch(t, more):
                    count = [0]

                    def link(ins):
                        count[0] += 1
                        ins.then_inc(s_calc, 1)
                        v.wait_ge(s_calc, t * STEPS_V + count[0])

                    v.wait_ge(s_go, t + 1)
                    col = bass.ds(t, 1)
                    link(nc.vector.tensor_copy(wide[:, :], m.dst_sb[:, col].to_broadcast([P, P])))
                    v.sem_inc(s_wide, 1)
                    nc.vector.tensor_copy(one_src[:, :], m.src_sb[:, col])
                    nc.vector.tensor_copy(one_w[:, :], m.w_sb[:, col])
                    nc.vector.tensor_copy(key[:, :], m.dst_sb[:, col]).then_inc(s_key, 1)
                    v.wait_ge(s_acr, t + 1)
                    link(nc.vector.tensor_scalar(same[:, :], across[:, :], wide[:, 0:1], None, ALU.is_equal))
                    link(nc.vector.reduce_sum(total[:, :], same[:, :], AX.X))
                    link(nc.vector.tensor_tensor(sameb[:, :], same[:, :], lower[:, :], ALU.mult))
                    link(nc.vector.reduce_sum(prior[:, :], sameb[:, :], AX.X))
                    v.wait_ge(s_base, (t + 1) * 16)
                    nc.vector.tensor_tensor(rank[:, :], base[:, :], prior[:, :], ALU.add)
                    nc.vector.tensor_tensor(nxt[:, :], base[:, :], total[:, :], ALU.add)
                    link(nc.vector.tensor_tensor(skip[:, :], total[:, :], prior[:, :], ALU.subtract))
                    link(nc.vector.tensor_scalar(skip[:, :], skip[:, :], -1.0, SKIP, ALU.add, ALU.mult))
                    nc.vector.tensor_tensor(nkey[:, :], skip[:, :], wide[:, 0:1], ALU.add).then_inc(s_rank, 1)
                    assert count[0] == STEPS_V

                columns(v, rank_batch)

        @block.tensor
        def _(pe):
            with pe.If(pe.value_load(m.unsorted[0:1, 0:1]) != 0):
                def turn(t, more):
                    pe.wait_ge(s_wide, t + 1)
                    nc.tensor.transpose(across[:, :], wide[:, :], m.ident[:, :]).then_inc(s_acr, 1)

                columns(pe, turn)


def phase_pack(nc, m):
    with ExitStack() as ctx:
        def sb(name, shape, dt=F32):
            return ctx.enter_context(nc.sbuf_tensor(name, shape, dt))

        def sem(name):
            return ctx.enter_context(nc.semaphore(name))

        part = sb("part2", [P, EW], I32)
        pack = sb("pack", [P, EW, 3])
        flag = sb("flag", [P, EW])
        maskb = sb("maskb", [P, EW], BF16)
        s_vec, s_packed, s_mask, s_out = (sem(n) for n in ("vec2", "packed_rdy", "mask_rdy", "stored2"))
        block = ctx.enter_context(nc.Block())

        @block.sync
        def _(sp):
            sp.wait_ge(s_packed, 3)
            sp.dma_start(m.packed.rearrange("(p r) c -> p (r c)", p=P),
                         pack[:, :, :].rearrange("p e c -> p (e c)")).then_inc(s_out, 16)
            sp.wait_ge(s_mask, 1)
            sp.dma_start(m.mask, maskb[:, :]).then_inc(s_out, 16)
            sp.wait_ge(s_out, 32)

        @block.vector
        def _(v):
            link = Chain(v, s_vec)
            dst, src = m.dst_sb, m.src_sb
            link(nc.vector.tensor_scalar(part[:, :], src[:, :], NB - 1, None, ALU.bitwise_and))
            nc.vector.tensor_copy(pack[:, :, 0], part[:, :]).then_inc(s_packed, 1)
            v.wait_ge(s_packed, 1)
            link(nc.vector.tensor_scalar(part[:, :], src[:, :], 7, None, ALU.arith_shift_right))
            nc.vector.scalar_tensor_tensor(out=pack[:, :, 1], in0=dst[:, :], scalar=float(NA), in1=part[:, :],
                                           op0=ALU.mult, op1=ALU.add).then_inc(s_packed, 1)
            nc.vector.tensor_copy(pack[:, :, 2], m.w_sb[:, :]).then_inc(s_packed, 1)
            link(nc.vector.tensor_tensor(flag[:, 1:EW], dst[:, 1:EW], dst[:, 0:EW - 1], ALU.not_equal))
            link(nc.vector.tensor_tensor(flag[:, 0:1], dst[:, 0:1], m.before[:, :], ALU.not_equal))
            nc.vector.tensor_scalar(maskb[:, :], flag[:, :], FAR, None, ALU.mult).then_inc(s_mask, 1)


def phase_adjacency(nc, m):
    with ExitStack() as ctx:
        def sb(name, shape, dt=F32):
            return ctx.enter_context(nc.sbuf_tensor(name, shape, dt))

        def sem(name):
            return ctx.enter_context(nc.semaphore(name))

        lo = sb("lo", [NP, GT], I32)
        rowi = sb("rowi", [NP, GT], I32)
        widx = sb("widx", [NP, GT, WR], I32)
        nb = sb("nb", [NP, NT], I32)
        ne = sb("ne", [NP, NT], I32)
        hi = sb("hi", [NP, GT], I32)
        used = sb("used", [NP, GT])
        over = sb("over", [NP, GT])
        overs = sb("overs", [NP, 1])
        has = sb("has", [NP, NT])
        last = sb("last", [NP, NT])
        win = sb("win", [NP, GT, WR * 3 * ROW])
        goff_i = sb("goff_i", [P, NG], I32)
        goff = sb("goff", [P, NG])
        cols = [sb(f"col{c}", [P, NG * HALF]) for c in range(3)]
        RING = 10
        oh_m = [sb(f"oh_m{r}", [P, NP]) for r in range(RING)]
        oh_w = [sb(f"oh_w{r}", [P, NB]) for r in range(RING)]
        rows = sb("rows", [NP, 2, GK, NB])
        pt = [ctx.enter_context(nc.psum_tensor(f"pt{k}", [P, 512], F32)) for k in range(8)]

        s_ld, s_dv, s_gidx, s_gidx2, s_win = sem("ends_in"), sem("dve_chain"), sem("goff_rdy"), sem("widx_rdy"), sem("win_in")
        s_over, s_crowd = sem("over_rdy"), sem("crowd_rdy")
        s_tr, s_ev, s_cols = sem("slots_up"), sem("slots_out"), sem("cols_rdy")
        s_ohr, s_free, s_done, s_evd = sem("oh_rdy"), sem("oh_free"), sem("bank_done"), sem("bank_free")
        s_rfree, s_rr = [sem(f"rows_stored{k}") for k in range(2)], sem("rows_rdy")
        block = ctx.enter_context(nc.Block())
        BANKS = [4] * 6 + [1]
        NBK = len(BANKS)
        CUT = 112

        @block.sync
        def _(sp):
            with nc.allow_non_contiguous_dma(reason="one count per group or node"):
                sp.dma_start(lo[:, :], m.ends[0:N].rearrange("(t p g) -> p t g", p=NP, g=G)[:, :, 0]).then_inc(s_ld, 16)
                sp.dma_start(hi[:, :], m.ends[G:N + G].rearrange("(t p g) -> p t g", p=NP, g=G)[:, :, 0]).then_inc(s_ld, 16)
                sp.dma_start(nb[:, :], m.ends[0:N].rearrange("(k p) -> p k", p=NP)).then_inc(s_ld, 16)
                sp.dma_start(ne[:, :], m.ends[1:1 + N].rearrange("(k p) -> p k", p=NP)).then_inc(s_ld, 16)
            out = m.adj.rearrange("d (a b) -> (d a) b", b=NB).rearrange("(q m) b -> m q b", m=NP)

            def store(k, t, parity):
                at = t * GK if isinstance(t, int) else sp.snap(t * GK)
                sp.wait_ge(s_rr, (t + 1) * NBK)
                for p0, p1 in ((0, CUT), (CUT, NP)):
                    sp.dma_start(out[p0:p1, bass.ds(at, GK), :],
                                 rows[p0:p1, parity, :, :]).then_inc(s_rfree[parity], 16)

            with sp.Fori(0, NT // 2) as i:
                for k in range(2):
                    store(k, i * 2 + k, k)
            store(0, NT - 1, 0)
            sp.wait_ge(s_rfree[0], 32 * (NT // 2 + 1))
            sp.wait_ge(s_rfree[1], 32 * (NT // 2))

        @block.gpsimd
        def _(g):
            nc.gpsimd.iota(goff_i[:, :], pattern=[[NP, NG]], base=0, channel_multiplier=0).then_inc(s_gidx, 1)
            g.wait_ge(s_gidx2, 1)
            for t in range(GT):
                for r in range(WR):
                    g.indirect_dma_start(win[:, t, r * 3 * ROW:(r + 1) * 3 * ROW], None, m.packed,
                                         bass.IndirectOffsetOnAxis(ap=widx[:, t, r:r + 1], axis=0)).then_inc(s_win, 16)
            g.wait_ge(s_win, 16 * GT * WR)

        @block.vector
        def _(v):
            link = Chain(v, s_dv)
            v.wait_ge(s_ld, 64)
            link(nc.vector.tensor_scalar(rowi[:, :], lo[:, :], 5, None, ALU.arith_shift_right))
            for r in range(WR):
                w = nc.vector.tensor_scalar(widx[:, :, r], rowi[:, :], float(r), None, ALU.add)
            w.then_inc(s_gidx2, 1)
            link(nc.vector.tensor_scalar(used[:, :], rowi[:, :], float(-ROW), None, ALU.mult))
            link(nc.vector.tensor_tensor(used[:, :], used[:, :], hi[:, :], ALU.add))
            link(nc.vector.tensor_scalar(over[:, :], used[:, :], float(WIN), None, ALU.is_gt))
            nc.vector.reduce_sum(overs[:, :], over[:, :], AX.X).then_inc(s_over, 1)
            zero_row = float(NC * CH)
            link(nc.vector.tensor_tensor(has[:, :], ne[:, :], nb[:, :], ALU.is_gt))
            link(nc.vector.tensor_scalar(last[:, :], ne[:, :], -1.0 - zero_row, None, ALU.add))
            link(nc.vector.tensor_tensor(last[:, :], last[:, :], has[:, :], ALU.mult))
            link(nc.vector.tensor_scalar(m.end_idx[:, :], last[:, :], zero_row, None, ALU.add))
            v.wait_ge(s_crowd, 1)
            link(nc.vector.tensor_copy(m.crowded[:, :], pt[7][0:1, 0:1]))
            v.wait_ge(s_gidx, 1)
            link(nc.vector.tensor_copy(goff[:, :], goff_i[:, :]))
            n = 0
            for t in range(GT):
                for h in range(HALF):
                    for c in range(3):
                        n += 1
                        v.wait_ge(s_tr, n)
                        dst = cols[c][:, :].rearrange("p (t q h) -> p t h q", t=GT, h=HALF)[:, t, h, :]
                        up = pt[(n - 1) % 4][:, 0:NP]
                        if c == 1:
                            nc.vector.tensor_tensor(dst, up, goff[:, t * NP:(t + 1) * NP], ALU.subtract).then_inc(s_ev, 1)
                        else:
                            nc.vector.tensor_copy(dst, up).then_inc(s_ev, 1)
            v.wait_ge(s_ev, n)
            with v.Fori(0, NT) as i:
                for s in range(STEPS):
                    r = s % RING
                    v.wait_ge(s_free, i * STEPS + s + 1)
                    c = bass.ds(i * STEPS + s, 1)
                    nc.vector.tensor_scalar(oh_m[r][:, :], m.iota[:, 0:NP], cols[1][:, c], None,
                                            ALU.is_equal).then_inc(s_ohr, 1)
                    nc.vector.tensor_scalar(oh_w[r][:, :], m.iota[:, :], cols[0][:, c], cols[2][:, c],
                                            ALU.is_equal, ALU.mult).then_inc(s_ohr, 1)

        @block.scalar
        def _(act):
            def evict(t, parity):
                q = 0
                for k, n in enumerate(BANKS):
                    act.wait_ge(s_done, t * NBK + k + 1)
                    nc.scalar.copy(rows[:, parity, q:q + n, :], pt[k][0:NP, 0:n * NB].rearrange("p (q b) -> p q b", b=NB))\
                        .then_inc(s_rr, 1)
                    q += n

            for t in range(2):
                evict(t, t)
            with act.Fori(1, NT // 2) as i:
                for k in range(2):
                    act.wait_ge(s_rfree[k], i * 32)
                    evict(i * 2 + k, k)
            act.wait_ge(s_rfree[0], 32 * (NT // 2))
            evict(NT - 1, 0)

        @block.tensor
        def _(pe):
            pe.sem_inc(s_free, RING)
            pe.wait_ge(s_over, 1)
            nc.tensor.matmul(pt[7][0:1, 0:1], overs[:, :], m.ones[0:NP, :], start=True, stop=True).then_inc(s_crowd, 1)
            n = 0
            pe.wait_ge(s_win, 16 * GT * WR)
            for t in range(GT):
                for h in range(HALF):
                    wv = win[:, t, :].rearrange("p (s c) -> p c s", c=3)
                    for c in range(3):
                        if n >= 4:
                            pe.wait_ge(s_ev, n - 3)
                        nc.tensor.transpose(pt[n % 4][:, 0:NP], wv[:, c, P * h:P * h + P],
                                            m.ident[0:NP, 0:NP]).then_inc(s_tr, 1)
                        n += 1
            pe.wait_ge(s_ev, n)

            def tile_of_groups(t, first):
                s = 0
                for k, groups in enumerate(BANKS):
                    if not first:
                        pe.wait_ge(s_rr, (t - 1) * NBK + k + 1)
                    for q in range(groups):
                        for h in range(HALF):
                            r = s % RING
                            pe.wait_ge(s_ohr, (t * STEPS + s + 1) * 2)
                            mm = nc.tensor.matmul(pt[k][0:NP, q * NB:(q + 1) * NB], oh_m[r][:, :], oh_w[r][:, :],
                                                  start=h == 0, stop=h == HALF - 1)
                            mm.then_inc(s_free, 1)
                            s += 1
                    pe.wait_ge(s_free, t * STEPS + s + RING)
                    pe.sem_inc(s_done, 1)

            tile_of_groups(0, True)
            with pe.Fori(1, NT) as i:
                tile_of_groups(i, False)


def phase_crowded(nc, m):
    with ExitStack() as ctx:
        def sb(name, shape, dt=F32):
            return ctx.enter_context(nc.sbuf_tensor(name, shape, dt))

        def sem(name):
            return ctx.enter_context(nc.semaphore(name))

        blank = sb("blank", [NP, SPAD])
        spot = sb("spot", [P, EW])
        upper = sb("upper", [P, P])
        wide = sb("wide_k", [P, P])
        wide_w = sb("wide_w", [P, P])
        same = sb("same_k", [P, P])
        later = sb("later", [P, P])
        share = sb("share", [P, P])
        key = sb("key_k", [P, 1], I32)
        nkey = sb("nkey_k", [P, 1], I32)
        old = sb("old", [P, 1])
        new = sb("new", [P, 1])
        sums = sb("sums", [P, 1])
        skip = sb("skip_k", [P, 1])
        across = ctx.enter_context(nc.psum_tensor("across_k", [P, P], F32))
        across_w = ctx.enter_context(nc.psum_tensor("across_w", [P, P], F32))
        s_up0, s_up, s_blank, s_zero, s_go, s_key, s_wide, s_acr, s_old, s_calc, s_new, s_put, s_dv = (
            sem(n) for n in ("upper_set", "upper_rdy", "blank_rdy", "zeroed", "batch_go_k", "key_rdy_k", "wide_rdy_k",
                             "across_rdy_k", "old_in", "calc_k", "new_rdy", "put_k", "spot_chain"))
        block = ctx.enter_context(nc.Block())
        CELLS = N * SPAD
        cells = m.adj.rearrange("d s -> (d s)").unsqueeze(1)

        @block.sync
        def _(sp):
            with sp.If(sp.value_load(m.crowded[0:1, 0:1]) != 0):
                sp.wait_ge(s_blank, 1)
                for k in range(NT):
                    sp.dma_start(m.adj[k * NP:(k + 1) * NP, :], blank[:, :]).then_inc(s_zero, 16)
                sp.wait_ge(s_zero, 16 * NT)

        @block.gpsimd
        def _(g):
            with g.If(g.value_load(m.crowded[0:1, 0:1]) != 0):
                nc.gpsimd.memset(upper[:, :], 1.0).then_inc(s_up0, 1)
                g.wait_ge(s_up0, 1)
                nc.gpsimd.affine_select(out=upper[:, :], in_=upper[:, :], compare_op=ALU.is_gt, fill=0.0, base=0,
                                        pattern=[[1, P]], channel_multiplier=-1).then_inc(s_up, 1)
                g.wait_ge(s_up, 1)
                g.wait_ge(s_zero, 16 * NT)
                g.sem_inc(s_go, 1)
                with g.Fori(0, EW) as t:
                    g.wait_ge(s_key, t + 1)
                    g.nop(nofuse=True)
                    g.indirect_dma_start(old[:, :], None, cells,
                                         bass.IndirectOffsetOnAxis(ap=key[:, :], axis=0)).then_inc(s_old, 16)
                    g.wait_ge(s_new, t + 1)
                    g.nop(nofuse=True)
                    g.indirect_dma_start(cells, bass.IndirectOffsetOnAxis(ap=nkey[:, :], axis=0), new[:, :], None,
                                         bounds_check=CELLS - 1, oob_is_err=False).then_inc(s_put, 16)
                    g.wait_ge(s_put, (t + 1) * 16)
                    g.nop(nofuse=True)
                    g.sem_inc(s_go, 1)

        @block.vector
        def _(v):
            with v.If(v.value_load(m.crowded[0:1, 0:1]) != 0):
                first = Chain(v, s_dv)
                nc.vector.memset(blank[:, :], 0.0).then_inc(s_blank, 1)
                first(nc.vector.scalar_tensor_tensor(out=spot[:, :], in0=m.dst_sb[:, :], scalar=float(SPAD),
                                                     in1=m.src_sb[:, :], op0=ALU.mult, op1=ALU.add))
                first(nc.vector.tensor_scalar(spot[:, :], spot[:, :], float(CELLS - 1), None, ALU.min))
                STEPS_V = 9
                with v.Fori(0, EW) as t:
                    count = [0]

                    def link(ins):
                        count[0] += 1
                        ins.then_inc(s_calc, 1)
                        v.wait_ge(s_calc, t * STEPS_V + count[0])

                    v.wait_ge(s_go, t + 1)
                    col = bass.ds(t, 1)
                    link(nc.vector.tensor_copy(wide[:, :], spot[:, col].to_broadcast([P, P])))
                    link(nc.vector.tensor_copy(wide_w[:, :], m.w_sb[:, col].to_broadcast([P, P])))
                    v.sem_inc(s_wide, 1)
                    nc.vector.tensor_copy(key[:, :], spot[:, col]).then_inc(s_key, 1)
                    v.wait_ge(s_acr, (t + 1) * 2)
                    link(nc.vector.tensor_scalar(same[:, :], across[:, :], wide[:, 0:1], None, ALU.is_equal))
                    link(nc.vector.tensor_tensor(share[:, :], same[:, :], across_w[:, :], ALU.mult))
                    link(nc.vector.reduce_sum(sums[:, :], share[:, :], AX.X))
                    link(nc.vector.tensor_tensor(later[:, :], same[:, :], upper[:, :], ALU.mult))
                    link(nc.vector.reduce_sum(skip[:, :], later[:, :], AX.X))
                    link(nc.vector.tensor_scalar(skip[:, :], skip[:, :], SKIP, None, ALU.mult))
                    v.wait_ge(s_old, (t + 1) * 16)
                    link(nc.vector.tensor_tensor(new[:, :], old[:, :], sums[:, :], ALU.add))
                    nc.vector.tensor_tensor(nkey[:, :], skip[:, :], wide[:, 0:1], ALU.add).then_inc(s_new, 1)
                    assert count[0] == STEPS_V

        @block.tensor
        def _(pe):
            with pe.If(pe.value_load(m.crowded[0:1, 0:1]) != 0):
                with pe.Fori(0, EW) as t:
                    pe.wait_ge(s_wide, t + 1)
                    nc.tensor.transpose(across[:, :], wide[:, :], m.ident[:, :]).then_inc(s_acr, 1)
                    nc.tensor.transpose(across_w[:, :], wide_w[:, :], m.ident[:, :]).then_inc(s_acr, 1)


def layer_norm(nc, link, x, tmp, stats, out, eps, s_go, s_back, v):
    shape = [NP, NT, D]
    mean, var = stats[:, 0, :], stats[:, 1, :]
    link(nc.vector.reduce_sum(mean, x, AX.X))
    link(nc.vector.tensor_scalar(mean, mean, 1.0 / D, None, ALU.mult))
    link(nc.vector.tensor_tensor(x, x, mean.unsqueeze(2).to_broadcast(shape), ALU.subtract))
    link(nc.vector.tensor_tensor(tmp, x, x, ALU.mult))
    link(nc.vector.reduce_sum(var, tmp, AX.X))
    nc.vector.tensor_scalar(var, var, 1.0 / D, None, ALU.mult).then_inc(s_go, 1)
    v.wait_ge(s_back, 1)
    link(nc.vector.reciprocal(var, var))
    link(nc.vector.tensor_tensor(out, x, var.unsqueeze(2).to_broadcast(shape), ALU.mult))


def phase_propagate(nc, m):
    with ExitStack() as ctx:
        def sb(name, shape, dt=F32):
            return ctx.enter_context(nc.sbuf_tensor(name, shape, dt))

        def sem(name):
            return ctx.enter_context(nc.semaphore(name))

        UK = 5
        ego = sb("ego", [NP, NT, D])
        acc = sb("acc", [NP, NT, D])
        tmp = sb("tmp", [NP, NT, D])
        stats = sb("stats", [NP, 2, NT])
        slot = [sb(f"slot{k}", [NP, D]) for k in range(UK)]
        at = [sb(f"at{k}", [NP, SPAD]) for k in range(UK)]
        agg_t = sb("agg_t", [D, SPAD])
        pa = [ctx.enter_context(nc.psum_tensor(f"pa{k}", [P, 512], F32)) for k in range(8)]
        s_at = [sem(f"adj_in{k}") for k in range(UK)]
        s_afree, s_init, s_slot, s_agg, s_out, s_tr, s_upd, s_ln, s_rt, s_dv = (
            sem(n) for n in ("adj_free", "ego_init", "slot_rdy", "agg_done", "agg_out", "turned", "updated", "ln_var", "ln_root",
                             "dve_chain2"))
        block = ctx.enter_context(nc.Block())
        SEG = [(512 * b, min(512, SPAD - 512 * b)) for b in range(-(-SPAD // 512))]
        TB = 5

        @block.sync
        def _(sp):
            with sp.Fori(0, ROUNDS * NT // UK) as i:
                for k in range(UK):
                    rows = [(sp.snap(((i * UK + k) % NT) * NP + p0), p0, p1) for p0, p1 in ((0, 112), (112, NP))]
                    sp.wait_ge(s_afree, i * UK + k + 1)
                    for row, p0, p1 in rows:
                        sp.dma_start(at[k][p0:p1, :], m.adj[bass.ds(row, p1 - p0), :]).then_inc(s_at[k], 16)

        @block.vector
        def _(v):
            link = Chain(v, s_dv)
            link(nc.vector.tensor_copy(ego[:, :, :], m.x[:, :, :]))
            link(nc.vector.tensor_copy(acc[:, :, :], m.x[:, :, :]))
            with v.Fori(0, ROUNDS) as r:
                with v.Fori(0, NT // UK) as i:
                    for k in range(UK):
                        n = r * NT + i * UK + k
                        v.wait_ge(s_afree, n + 1)
                        nc.vector.tensor_copy(slot[k][:, :], ego[:, bass.ds(i * UK + k, 1), :].rearrange("p a d -> p (a d)"))\
                            .then_inc(s_slot, 1)
                for b in range(NT // TB):
                    v.wait_ge(s_tr, r * (NT // TB) + b + 1)
                    e = ego[:, b * TB:(b + 1) * TB, :]
                    g = pa[b][0:NP, 0:TB * D].rearrange("p (k d) -> p k d", d=D)
                    nc.vector.scalar_tensor_tensor(out=e, in0=e, scalar=1.0, in1=g, op0=ALU.add, op1=ALU.mult)\
                        .then_inc(s_upd, 1)
                v.wait_ge(s_upd, (r * 2 + 1) * (NT // TB))
                for b in range(NT // TB):
                    e, a = (t[:, b * TB:(b + 1) * TB, :] for t in (ego, acc))
                    nc.vector.tensor_tensor(a, a, e, ALU.add).then_inc(s_upd, 1)
                v.wait_ge(s_upd, (r + 1) * 2 * (NT // TB))
            link(nc.vector.scalar_tensor_tensor(out=acc[:, :, :], in0=acc[:, :, :], scalar=1.0 / (ROUNDS + 1),
                                                in1=m.x[:, :, :], op0=ALU.mult, op1=ALU.add))
            layer_norm(nc, link, acc[:, :, :], tmp[:, :, :], stats, m.x[:, :, :], m.eps, s_ln, s_rt, v)

        @block.scalar
        def _(act):
            with act.Fori(0, ROUNDS) as r:
                act.wait_ge(s_agg, r + 1)
                for b, (c0, w) in enumerate(SEG):
                    nc.scalar.copy(agg_t[:, c0:c0 + w], pa[b][0:D, 0:w]).then_inc(s_out, 1)
            act.wait_ge(s_ln, 1)
            nc.scalar.activation(stats[:, 1, :], stats[:, 1, :], ACT.Sqrt, bias=m.eps[:, :]).then_inc(s_rt, 1)

        @block.tensor
        def _(pe):
            pe.sem_inc(s_afree, UK)

            def product(r, t, k, first, last):
                n = r * NT + t
                pe.wait_ge(s_slot, n + 1)
                pe.wait_ge(s_at[k], (r * (NT // UK) + (t - k) // UK + 1) * 32)
                for b, (c0, w) in enumerate(SEG):
                    mm = nc.tensor.matmul(pa[b][0:D, 0:w], slot[k][:, :], at[k][:, c0:c0 + w], start=first, stop=last)
                mm.then_inc(s_afree, 1)

            with pe.Fori(0, ROUNDS) as r:
                for k in range(UK):
                    product(r, k, k, k == 0, False)
                with pe.Fori(1, NT // UK - 1) as i:
                    for k in range(UK):
                        n = r * NT + i * UK + k
                        pe.wait_ge(s_slot, n + 1)
                        pe.wait_ge(s_at[k], (r * (NT // UK) + i + 1) * 32)
                        for b, (c0, w) in enumerate(SEG):
                            mm = nc.tensor.matmul(pa[b][0:D, 0:w], slot[k][:, :], at[k][:, c0:c0 + w], start=False, stop=False)
                        mm.then_inc(s_afree, 1)
                for k in range(UK):
                    product(r, NT - UK + k, k, False, k == UK - 1)
                pe.wait_ge(s_afree, (r + 1) * NT + UK)
                pe.sem_inc(s_agg, 1)
                pe.wait_ge(s_out, (r + 1) * len(SEG))
                for b in range(NT // TB):
                    for j in range(TB):
                        t = b * TB + j
                        mm = nc.tensor.transpose(pa[b][0:NP, j * D:(j + 1) * D], agg_t[:, t * NP:(t + 1) * NP],
                                                 m.ident[0:D, 0:D])
                    mm.then_inc(s_tr, 1)
                pe.wait_ge(s_upd, (r * 2 + 1) * (NT // TB))


def phase_conv(nc, m, layer, x_in, w_msg, w_edge, w_root, bias, conv_out, final):
    with ExitStack() as ctx:
        def sb(name, shape, dt=F32):
            return ctx.enter_context(nc.sbuf_tensor(f"{name}_{layer}", shape, dt))

        def sem(name):
            return ctx.enter_context(nc.semaphore(f"{name}_{layer}"))

        U = 4
        V = 2
        wmr = sb("wmr", [D, 2 * D])
        we = sb("we", [P, 4, D])
        bb = sb("bb", [NP, D])
        xt = sb("xt", [D, N])
        y_sb = sb("y_sb", [NP, NT, D])
        z = sb("z", [NP, NT, D])
        agg = sb("agg", [NP, NT, D])
        tmp = sb("tmp", [NP, NT, D])
        stats = sb("stats", [NP, 2, NT])
        gi = [sb(f"gi{k}", [P, 4], I32) for k in range(U)]
        got = [sb(f"got{k}", [P, 4, D]) for k in range(U)]
        ea = [sb(f"ea{k}", [P, 4 * DE]) for k in range(U)]
        eat = [sb(f"eat{k}", [P, P]) for k in range(V)]
        mk = [sb(f"mk{k}", [D, CH], BF16) for k in range(U)]
        sc = [sb(f"sc{k}", [D, CH]) for k in range(U)]
        so = [sb(f"so{k}", [P, 4, D]) for k in range(U)]
        ps_m = [ctx.enter_context(nc.psum_tensor(f"ps_m{k}_{layer}", [P, 512], F32)) for k in range(U)]
        ps_e = [ctx.enter_context(nc.psum_tensor(f"ps_e{k}_{layer}", [P, 512], F32)) for k in range(V)]
        ps_o = [ctx.enter_context(nc.psum_tensor(f"ps_o{k}_{layer}", [P, 512], F32)) for k in range(V)]
        s_wl, s_wz, s_t, s_te, s_y, s_ye, s_ys = (
            sem(n) for n in ("w_in", "w_zero", "xt_up", "xt_out", "y_up", "y_out", "y_stored"))
        s_idx = sem("idx_staged")
        s_got = [sem(f"rows_in{k}") for k in range(U)]
        s_ea, s_mk = [sem(f"ea_in{k}") for k in range(U)], [sem(f"mask_in{k}") for k in range(U)]
        s_eup, s_eat, s_msg, s_scan, s_up, s_so = (
            sem(n) for n in ("ea_up", "eat_rdy", "msg_done", "scanned", "maxima_up", "maxima_out"))
        s_sw = [sem(f"seg_stored{k}") for k in range(U)]
        s_end, s_agg, s_dv, s_ln, s_rt, s_res = (
            sem(n) for n in ("all_stored", "agg_in", "chain", "var", "root", "result"))
        mask_c = m.mask.rearrange("p e -> (p e)")
        LOOPS = NC // U

        def over_chunks(eng, body):
            for k in range(U):
                body(0, k)
            with eng.Fori(1, LOOPS) as i:
                for k in range(U):
                    body(i, k)
            for k in range(NC - LOOPS * U):
                body(LOOPS, k)

        def step(i, k, ahead):
            k += ahead
            return i + k // U, k % U

        def known(i):
            return isinstance(i, int)

        block = ctx.enter_context(nc.Block())

        @block.sync
        def _(sp):
            sp.dma_start(wmr[:, 0:D], w_msg).then_inc(s_wl, 16)
            sp.dma_start(wmr[:, D:2 * D], w_root).then_inc(s_wl, 16)
            sp.dma_start(bb[:, :], bias.unsqueeze(0).to_broadcast([NP, D])).then_inc(s_wl, 16)
            sp.wait_ge(s_wz, 1)
            for j in range(4):
                sp.dma_start(we[j * DE:(j + 1) * DE, j, :], w_edge).then_inc(s_wl, 16)

            def load(i, k):
                c = i * U + k
                edge = c * CH if known(i) else sp.snap(c * CH)
                if not known(i) or i > 0:
                    sp.wait_ge(s_eup, c + 1 - U)
                if not known(i) or c < NC - 1:
                    sp.dma_start(ea[k][:, :], m.ea_s[bass.ds(edge, CH), :].rearrange("(p j) f -> p (j f)", j=4))\
                        .then_inc(s_ea[k], 16)
                else:
                    n = E - edge
                    sp.dma_start(ea[k][0:n // 4, :], m.ea_s[edge:edge + n // 4 * 4, :].rearrange("(p j) f -> p (j f)", j=4))\
                        .then_inc(s_ea[k], 16)
                    sp.dma_start(ea[k][n // 4:n // 4 + 1, 0:n % 4 * DE],
                                 m.ea_s[edge + n // 4 * 4:E, :].rearrange("(o j) f -> o (j f)", o=1)).then_inc(s_ea[k], 16)
                if not known(i) or i > 0:
                    sp.wait_ge(s_scan, c + 1 - U)
                    sp.nop(nofuse=True)
                sp.dma_start(mk[k][:, :], mask_c[bass.ds(edge, CH)].unsqueeze(0).to_broadcast([D, CH])).then_inc(s_mk[k], 16)

            over_chunks(sp, load)

        @block.gpsimd
        def _(g):
            nc.gpsimd.memset(we[:, :, :], 0.0).then_inc(s_wz, 1)
            g.wait_ge(s_ys, 16)

            def gather(i, k):
                g.wait_ge(s_idx, i * U + k + 1)
                g.nop(nofuse=True)
                for j in range(4):
                    g.indirect_dma_start(got[k][:, j, :], None, m.y,
                                         bass.IndirectOffsetOnAxis(ap=gi[k][:, j:j + 1], axis=0)).then_inc(s_got[k], 16)

            over_chunks(g, gather)
            g.wait_ge(s_end, 1)
            for t in range(NT):
                g.indirect_dma_start(agg[:, t, :], None, m.seg,
                                     bass.IndirectOffsetOnAxis(ap=m.end_idx[:, t:t + 1], axis=0)).then_inc(s_agg, 16)
            g.wait_ge(s_agg, 16 * NT)

        @block.vector
        def _(v):
            link = Chain(v, s_dv)

            def stage(i, k):
                nc.vector.tensor_copy(gi[k][:, :], m.src_idx[:, bass.ds((i * U + k) * 4, 4)]).then_inc(s_idx, 1)

            for k in range(U):
                stage(0, k)
            v.wait_ge(s_wl, 16 * 7)
            for t in range(NT):
                v.wait_ge(s_y, t + 1)
                bank = ps_o[t % 2]
                nc.vector.tensor_copy(y_sb[:, t, :], bank[0:NP, 0:D])
                nc.vector.tensor_tensor(z[:, t, :], bank[0:NP, D:2 * D], bb[:, :], ALU.add).then_inc(s_ye, 1)
            link(nc.vector.memset(sc[U - 1][:, CH - 1:CH], 0.0))

            def scan(i, k):
                c = i * U + k
                v.wait_ge(s_msg, c + 1)
                if not known(i) or i < LOOPS:
                    stage(i + 1, k)
                v.wait_ge(s_mk[k], (i + 1) * 16)
                if not known(i) or c > 0:
                    v.wait_ge(s_scan, c)
                if not known(i) or i > 0:
                    v.wait_ge(s_up, c + 1 - U)
                nc.vector.tensor_tensor_scan(sc[k][:, :], mk[k][:, :], ps_m[k][0:D, :], sc[k - 1][:, CH - 1:CH],
                                             ALU.add, ALU.max).then_inc(s_scan, 1)

            over_chunks(v, scan)
            v.wait_ge(s_agg, 16 * NT)
            link(nc.vector.tensor_tensor(z[:, :, :], z[:, :, :], agg[:, :, :], ALU.add))
            res = tmp if final else conv_out
            link(nc.vector.scalar_tensor_tensor(out=res[:, :, :], in0=z[:, :, :], scalar=SLOPE, in1=z[:, :, :],
                                                op0=ALU.mult, op1=ALU.max))
            if final:
                link(nc.vector.tensor_tensor(z[:, :, :], tmp[:, :, :], m.x[:, :, :], ALU.add))
                layer_norm(nc, link, z[:, :, :], tmp[:, :, :], stats, agg[:, :, :], m.eps, s_ln, s_rt, v)
                v.sem_inc(s_res, 1)

        @block.scalar
        def _(act):
            for t in range(NT):
                act.wait_ge(s_t, t + 1)
                nc.scalar.copy(xt[:, t * NP:(t + 1) * NP], ps_m[t % 2][0:D, 0:NP]).then_inc(s_te, 1)
            act.wait_ge(s_ye, NT)
            act.dma_start(m.y.rearrange("(k p) d -> p k d", p=NP), y_sb[:, :, :]).then_inc(s_ys, 16)
            act.wait_ge(s_ys, 16)

            def features_out(i, k):
                c = i * U + k
                act.wait_ge(s_eup, c + 1)
                if not known(i) or c >= V:
                    act.wait_ge(s_msg, c + 1 - V)
                nc.scalar.copy(eat[k % V][:, :], ps_e[k % V][:, 0:P]).then_inc(s_eat, 1)

            def maxima_out(i, k):
                c = i * U + k
                edge = c * CH if known(i) else act.snap(c * CH)
                act.wait_ge(s_up, c + 1)
                if not known(i) or i > 0:
                    act.wait_ge(s_sw[k], i * 16)
                nc.scalar.copy(so[k][:, :, :], ps_o[k % V][:, 0:4 * D].rearrange("p (j d) -> p j d", d=D)).then_inc(s_so, 1)
                act.wait_ge(s_so, c + 1)
                act.dma_start(m.seg[bass.ds(edge, CH), :].rearrange("(p j) d -> p (j d)", j=4),
                              so[k][:, :, :].rearrange("p j d -> p (j d)")).then_inc(s_sw[k], 16)

            features_out(0, 0)

            def chunk(i, k):
                if not known(i) or i * U + k < NC - 1:
                    features_out(*step(i, k, 1))
                if not known(i) or i * U + k > 0:
                    maxima_out(*step(i, k, -1))

            over_chunks(act, chunk)
            maxima_out(*step(LOOPS, NC % U, -1))
            for k in range(U):
                act.wait_ge(s_sw[k], (NC - k + U - 1) // U * 16)
            act.sem_inc(s_end, 1)
            if final:
                act.wait_ge(s_ln, 1)
                nc.scalar.activation(stats[:, 1, :], stats[:, 1, :], ACT.Sqrt, bias=m.eps[:, :]).then_inc(s_rt, 1)
                act.wait_ge(s_res, 1)
                act.dma_start(m.out.rearrange("(k p) d -> p k d", p=NP), agg[:, :, :]).then_inc(s_ys, 16)
                act.wait_ge(s_ys, 32)

        @block.tensor
        def _(pe):
            for t in range(NT):
                if t >= 2:
                    pe.wait_ge(s_te, t - 1)
                nc.tensor.transpose(ps_m[t % 2][0:D, 0:NP], x_in[:, t, :], m.ident[0:NP, 0:NP]).then_inc(s_t, 1)
            pe.wait_ge(s_te, NT)
            pe.wait_ge(s_wl, 16 * 7)
            for t in range(NT):
                if t >= 2:
                    pe.wait_ge(s_ye, t - 1)
                nc.tensor.matmul(ps_o[t % 2][0:NP, 0:2 * D], xt[:, t * NP:(t + 1) * NP], wmr[:, :],
                                 start=True, stop=True).then_inc(s_y, 1)
            pe.wait_ge(s_ye, NT)

            def turn_features(i, k):
                c = i * U + k
                parts = 2 if known(i) and c == NC - 1 else 1
                pe.wait_ge(s_ea[k], (i + parts) * 16)
                if not known(i) or c >= V:
                    pe.wait_ge(s_eat, c + 1 - V)
                nc.tensor.transpose(ps_e[k % V][:, 0:P], ea[k][:, :], m.ident[:, :]).then_inc(s_eup, 1)

            def messages(i, k):
                c = i * U + k
                pe.wait_ge(s_eat, c + 1)
                if not known(i) or i > 0:
                    pe.wait_ge(s_scan, c + 1 - U)
                cols = ps_m[k][0:D, :].rearrange("d (p j) -> d j p", j=4)
                for j in range(4):
                    nc.tensor.matmul(cols[:, j, :], we[:, j, :], eat[k % V][:, :], start=j == 0, stop=False,
                                     skip_group_check=True)
                pe.wait_ge(s_got[k], (i + 1) * 64)
                for j in range(4):
                    mm = nc.tensor.matmul(cols[:, j, :], got[k][:, j, :], m.ident[:, :], start=False, stop=j == 3,
                                          skip_group_check=True)
                mm.then_inc(s_msg, 1)

            def turn_maxima(i, k):
                c = i * U + k
                pe.wait_ge(s_scan, c + 1)
                if not known(i) or c >= V:
                    pe.wait_ge(s_so, c + 1 - V)
                cols = sc[k][:, :].rearrange("d (p j) -> d j p", j=4)
                for j in range(4):
                    mm = nc.tensor.transpose(ps_o[k % V][:, j * D:(j + 1) * D], cols[:, j, :], m.ident[0:D, 0:D])
                mm.then_inc(s_up, 1)

            turn_features(0, 0)

            def chunk(i, k):
                if not known(i) or i * U + k < NC - 1:
                    turn_features(*step(i, k, 1))
                messages(i, k)
                if not known(i) or i * U + k > 0:
                    turn_maxima(*step(i, k, -1))

            over_chunks(pe, chunk)
            turn_maxima(*step(LOOPS, NC % U, -1))


def gnn_program(nc, x, src, dst, edge_attr, edge_weight, weights, out):
    with ExitStack() as ctx:
        m = Mem()
        m.x_in, m.src, m.dst, m.ea, m.w, m.out = x, src, dst, edge_attr, edge_weight, out
        persistent(nc, ctx, m)
        phase_count(nc, m)
        phase_sort(nc, m)
        phase_pack(nc, m)
        phase_adjacency(nc, m)
        phase_crowded(nc, m)
        phase_propagate(nc, m)
        c1 = ctx.enter_context(nc.sbuf_tensor("c1", [NP, NT, D], F32))
        phase_conv(nc, m, 1, m.x, *weights[0:4], c1, False)
        phase_conv(nc, m, 2, c1, *weights[4:8], None, True)


_INS = ["x", "src", "dst", "edge_attr_32", "edge_weight",
        "L1_gnn_W1_msg", "L1_gnn_W1_edge", "L1_gnn_W1_root", "L1_gnn_b1",
        "L1_gnn_W2_msg", "L1_gnn_W2_edge", "L1_gnn_W2_root", "L1_gnn_b2"]


def kernel(**inputs):
    import numpy as np
    import concourse.bacc as bacc
    from concourse.bass_utils import run_bass_kernel_spmd as run

    nc = bacc.Bacc("TRN2", target_bir_lowering=False, num_devices=1)
    arrays, args = {}, []
    for name in _INS:
        a = np.ascontiguousarray(inputs[name])
        arrays[f"in_{name}"] = a
        args.append(nc.dram_tensor(f"in_{name}", a.shape, mybir.dt.from_np(a.dtype), kind="ExternalInput").ap())
    out = nc.dram_tensor("out_x", (N, D), F32, kind="ExternalOutput").ap()
    gnn_program(nc, *args[:5], args[5:], out)
    return run(nc, [arrays], core_ids=[0]).results[0]["out_x"]
```

```python
from contextlib import ExitStack

import concourse.bass as bass
from concourse import mybir

F32, BF16, I32 = mybir.dt.float32, mybir.dt.bfloat16, mybir.dt.int32
ALU, ACT, AX = mybir.AluOpType, mybir.ActivationFunctionType, mybir.AxisListType

P = 128
N, D, E, DE = 3125, 96, 103125, 32
ROUNDS = 3
EPS = 1e-5
SLOPE = 0.01

NB = 128
NA = -(-N // NB)
SPAD = NA * NB
CB = 64
CB_BITS = 6
CA = -(-(N + 1) // CB)
CPAD = CA * CB
NP = 125
NT = N // NP
G = NP // NA
NG = N // G
GT = NG // NP
GK = NP // G

CH = 512
NC = -(-E // CH)
ROW = 32
EW = 26 * ROW
EP = P * EW
PROWS = EP // ROW
WR = 8
WIN = WR * ROW
HALF = WIN // P
STEPS = GK * HALF
DPAD = N
SKIP = float(1 << 24)
FAR = -3.3e38


U = 4
PE_TILE = 3
PE_SLOTS = (1, 3)
PE_ROWS = EP // CH // U * len(PE_SLOTS)


def full_rows(width):
    return E // width, E % width


class Chain:

    def __init__(self, eng, sem):
        self.eng, self.sem, self.n = eng, sem, 0

    def __call__(self, ins):
        self.n += 1
        ins.then_inc(self.sem, 1)
        self.eng.wait_ge(self.sem, self.n)


class Mem:
    pass


def persistent(nc, ctx, m):
    def sb(name, shape, dt=F32):
        return ctx.enter_context(nc.sbuf_tensor(name, shape, dt))

    m.ident = sb("ident", [P, P])
    m.iota = sb("iota", [P, P])
    m.src_idx = sb("src_idx", [P, EP // P], I32)
    m.x = sb("x_nat", [NP, NT, D])
    m.end_idx = sb("end_idx", [NP, NT], I32)
    m.zero = sb("zero_row", [NP, D])
    m.ones = sb("ones", [P, 1])
    m.ramp = sb("ramp", [P, P], I32)
    m.unsorted = sb("unsorted", [1, 1], I32)
    m.crowded = sb("crowded", [1, 1], I32)
    m.dst_sb = sb("dst_sb", [P, EW], I32)
    m.src_sb = sb("src_sb", [P, EW], I32)
    m.w_sb = sb("w_sb", [P, EW])
    m.before = sb("before", [P, 1], I32)
    m.eps = sb("eps", [NP, 1])

    def dram(name, shape, dt=F32):
        return nc.dram_tensor(name, shape, dt, kind="Internal").ap()

    m.packed = dram("packed", (PROWS, 3 * ROW))
    m.mask = dram("mask", (P, EW), BF16)
    m.ends = dram("ends", (1 + CPAD,), I32)
    m.adj = dram("adj", (N, SPAD))
    m.src_s = dram("src_sorted", (EP,), I32)
    m.dst_s = dram("dst_sorted", (EP,), I32)
    m.w_s = dram("w_sorted", (EP,))
    m.ea_s = dram("ea_sorted", (EP, DE))
    m.pe_src = dram("pe_src", (PE_ROWS, P), mybir.dt.int16)
    m.place = dram("place", (CPAD,), I32)
    m.y = dram("y_rows", (N, D))
    m.seg = dram("seg", (NC * CH + 1, D))


def load_source_order(nc, m, eng, sem, src, padded):
    idx = m.src_idx[:, :].rearrange("p (c j) -> p c j", j=4)
    if padded:
        eng.dma_start(idx, src.rearrange("(c p j) -> p c j", p=P, j=4)).then_inc(sem, 16)
        return 16
    full, rest = full_rows(CH)
    eng.dma_start(idx[:, 0:full, :], src[0:full * CH].rearrange("(c p j) -> p c j", p=P, j=4)).then_inc(sem, 16)
    eng.dma_start(idx[0:rest // 4, full, :],
                  src[full * CH:E - rest % 4].rearrange("(p j) -> p j", j=4)).then_inc(sem, 16)
    eng.dma_start(idx[rest // 4:rest // 4 + 1, full, 0:rest % 4], src[E - rest % 4:E].unsqueeze(0)).then_inc(sem, 16)
    return 48


def phase_count(nc, m):
    with ExitStack() as ctx:
        def sb(name, shape, dt=F32):
            return ctx.enter_context(nc.sbuf_tensor(name, shape, dt))

        def sem(name):
            return ctx.enter_context(nc.semaphore(name))

        part = sb("part", [P, EW], I32)
        drop = sb("drop", [P, EW])
        drops = sb("drops", [P, 1])
        da = sb("da", [P, EW], BF16)
        db = sb("db", [P, EW], BF16)
        HT = 16
        iota_t = sb("iota_t", [P, CB, HT], BF16)
        oh_a = [sb(f"oh_a{k}", [P, CA, HT], BF16) for k in range(2)]
        oh_b = [sb(f"oh_b{k}", [P, CB, HT], BF16) for k in range(2)]
        cnt = sb("cnt", [CA, CB])
        run = sb("run", [CA, CB])
        zeros = sb("zeros", [CA, CB])
        ends_i = sb("ends_i", [CA, CB], I32)
        tri = sb("tri", [CA, CA])
        first = sb("first", [1, 1], I32)
        hist = ctx.enter_context(nc.psum_tensor("hist", [CA, CB], F32))
        carry = ctx.enter_context(nc.psum_tensor("carry", [CA, 1], F32))
        bad = ctx.enter_context(nc.psum_tensor("bad", [1, 1], F32))

        s_const, s_ramp, s_fill, s_load, s_vec = (sem(n) for n in ("const", "ramp_rdy", "filled", "loaded", "vec"))
        s_dst = sem("dst_in")
        s_oh, s_ohfree, s_drop, s_bad = (
            sem(n) for n in ("onehots_rdy", "onehots_free", "drops_rdy", "bad_rdy"))
        s_tot, s_carry, s_ends, s_out = sem("totals_rdy"), sem("carry_rdy"), sem("ends_rdy"), sem("stored")
        s_idx0 = sem("idx_cleared")
        s_gz, s_order, s_ea = sem("pool_chain"), sem("ordered_in"), sem("ea_copied")
        block = ctx.enter_context(nc.Block())
        full, rest = full_rows(EW)
        LOADS = 6

        @block.sync
        def _(sp):
            def load(buf, arr, sem):
                sp.dma_start(buf[0:full, :], arr[0:full * EW].rearrange("(p e) -> p e", e=EW)).then_inc(sem, 16)
                sp.dma_start(buf[full:full + 1, 0:rest], arr[full * EW:E].unsqueeze(0)).then_inc(sem, 16)

            sp.wait_ge(s_fill, 2)
            load(m.dst_sb, m.dst, s_dst)
            with nc.allow_non_contiguous_dma(reason="one neighbour per partition"):
                sp.dma_start(m.before[1:full + 1, :],
                             m.dst[0:full * EW].rearrange("(p e) -> p e", e=EW)[:, EW - 1:EW]).then_inc(s_dst, 16)
            sp.wait_ge(s_fill, 4)
            load(m.src_sb, m.src, s_load)
            load(m.w_sb, m.w, s_load)
            sp.dma_start(m.x[:, :, :], m.x_in.rearrange("(k p) d -> p k d", p=NP)).then_inc(s_load, 16)
            sp.dma_start(m.seg[NC * CH:NC * CH + 1, :], m.zero[0:1, :]).then_inc(s_load, 16)
            sp.wait_ge(s_ends, 1)
            sp.dma_start(m.ends[1:1 + CPAD].rearrange("(a b) -> a b", b=CB), ends_i[:, :]).then_inc(s_out, 16)
            sp.dma_start(m.ends[0:1].unsqueeze(0), first[:, :]).then_inc(s_out, 16)
            sp.wait_ge(s_out, 32)
            sp.wait_ge(s_load, 16 * LOADS)

        @block.gpsimd
        def _(g):
            nc.gpsimd.memset(m.src_idx[:, :], 0).then_inc(s_idx0, 1)
            nc.gpsimd.iota(m.ramp[:, :], pattern=[[1, P]], base=0, channel_multiplier=0).then_inc(s_ramp, 1)
            nc.gpsimd.memset(m.ident[:, :], 0.0).then_inc(s_gz, 1)
            nc.gpsimd.memset(tri[:, :], 1.0).then_inc(s_gz, 1)
            g.wait_ge(s_gz, 2)
            nc.gpsimd.affine_select(out=m.ident[:, :], in_=m.ident[:, :], compare_op=ALU.not_equal, fill=1.0, base=0,
                                    pattern=[[-1, P]], channel_multiplier=1).then_inc(s_const, 1)
            nc.gpsimd.affine_select(out=tri[:, :], in_=tri[:, :], compare_op=ALU.is_gt, fill=0.0, base=0,
                                    pattern=[[1, CA]], channel_multiplier=-1).then_inc(s_const, 1)
        @block.scalar
        def _(act):
            act.wait_ge(s_idx0, 1)
            n = load_source_order(nc, m, act, s_order, m.src, False)
            act.dma_start(m.ea_s[0:E, :].rearrange("(p e) f -> p (e f)", p=NP), m.ea.rearrange("(p e) f -> p (e f)", p=NP))\
                .then_inc(s_ea, 16)
            act.wait_ge(s_order, n)
            act.wait_ge(s_ea, 16)

        @block.vector
        def _(v):
            link = Chain(v, s_vec)
            nc.vector.memset(m.dst_sb[:, :], DPAD).then_inc(s_fill, 1)
            nc.vector.memset(m.before[:, :], -1).then_inc(s_fill, 1)
            nc.vector.memset(m.src_sb[:, :], 0).then_inc(s_fill, 1)
            nc.vector.memset(m.zero[:, :], 0.0)
            nc.vector.memset(m.w_sb[:, :], 0.0).then_inc(s_fill, 1)
            for buf, value in ((m.eps, EPS), (m.ones, 1.0), (first, 0), (zeros, 0.0)):
                nc.vector.memset(buf[:, :], value)
            v.wait_ge(s_ramp, 1)
            link(nc.vector.tensor_copy(m.iota[:, :], m.ramp[:, :]))
            link(nc.vector.tensor_copy(iota_t[:, :, :], m.iota[:, 0:CB].unsqueeze(2).to_broadcast([P, CB, HT])))
            v.wait_ge(s_dst, 48)
            dst = m.dst_sb
            link(nc.vector.tensor_scalar(part[:, :], dst[:, :], CB_BITS, None, ALU.arith_shift_right))
            link(nc.vector.tensor_copy(da[:, :], part[:, :]))
            link(nc.vector.tensor_scalar(part[:, :], dst[:, :], CB - 1, None, ALU.bitwise_and))
            link(nc.vector.tensor_copy(db[:, :], part[:, :]))
            with v.Fori(0, EW // HT // 2) as i:
                for k in range(2):
                    v.wait_ge(s_ohfree, i * 2 + k + 1)
                    nc.vector.tensor_tensor(oh_a[k][:, :, :], iota_t[:, 0:CA, :],
                                            da[:, bass.ds((i * 2 + k) * HT, HT)].unsqueeze(1).to_broadcast([P, CA, HT]),
                                            ALU.is_equal).then_inc(s_oh, 1)
                    nc.vector.tensor_tensor(oh_b[k][:, :, :], iota_t[:, :, :],
                                            db[:, bass.ds((i * 2 + k) * HT, HT)].unsqueeze(1).to_broadcast([P, CB, HT]),
                                            ALU.is_equal).then_inc(s_oh, 1)
            link(nc.vector.tensor_tensor(drop[:, 1:EW], dst[:, 1:EW], dst[:, 0:EW - 1], ALU.is_lt))
            link(nc.vector.tensor_tensor(drop[:, 0:1], dst[:, 0:1], m.before[:, :], ALU.is_lt))
            nc.vector.tensor_reduce(drops[:, :], drop[:, :], AX.X, ALU.max).then_inc(s_drop, 1)
            v.wait_ge(s_ohfree, EW // HT + 2)
            link(nc.vector.tensor_copy(cnt[:, :], hist[:, :]))
            nc.vector.tensor_tensor_scan(run[:, :], cnt[:, :], zeros[:, :], 0.0, ALU.add, ALU.add).then_inc(s_tot, 1)
            v.wait_ge(s_carry, 1)
            nc.vector.tensor_scalar(ends_i[:, :], run[:, :], carry[:, 0:1], None, ALU.add).then_inc(s_ends, 1)
            v.wait_ge(s_bad, 1)
            link(nc.vector.tensor_copy(m.unsorted[:, :], bad[:, :]))

        @block.tensor
        def _(pe):
            pe.sem_inc(s_ohfree, 2)
            n_slots = EW // HT

            def count(k, slot, first, last):
                pe.wait_ge(s_oh, (slot + 1) * 2)
                for t in range(HT):
                    mm = nc.tensor.matmul(hist[:, :], oh_a[k][:, :, t], oh_b[k][:, :, t],
                                          start=first and t == 0, stop=last and t == HT - 1)
                mm.then_inc(s_ohfree, 1)

            count(0, 0, True, False)
            count(1, 1, False, False)
            with pe.Fori(1, n_slots // 2 - 1) as i:
                for k in range(2):
                    count(k, i * 2 + k, False, False)
            count(0, n_slots - 2, False, False)
            count(1, n_slots - 1, False, True)
            pe.wait_ge(s_drop, 1)
            nc.tensor.matmul(bad[:, :], drops[:, :], m.ones[:, :], start=True, stop=True).then_inc(s_bad, 1)
            pe.wait_ge(s_tot, 1)
            pe.wait_ge(s_const, 2)
            nc.tensor.matmul(carry[:, :], tri[:, :], run[:, CB - 1:CB], start=True, stop=True).then_inc(s_carry, 1)


def phase_sort(nc, m):
    with ExitStack() as ctx:
        def sb(name, shape, dt=F32):
            return ctx.enter_context(nc.sbuf_tensor(name, shape, dt))

        def sem(name):
            return ctx.enter_context(nc.semaphore(name))

        lower = sb("lower", [P, P])
        wide = sb("wide", [P, P])
        same = sb("same", [P, P])
        sameb = sb("sameb", [P, P])
        key = sb("key", [P, 1], I32)
        one_src = sb("one_src", [P, 1], I32)
        one_w = sb("one_w", [P, 1])
        one_ea = sb("one_ea", [P, DE])
        base = sb("base", [P, 1], I32)
        prior = sb("prior", [P, 1])
        total = sb("total", [P, 1])
        skip = sb("skip", [P, 1])
        rank = sb("rank", [P, 1], I32)
        nxt = sb("nxt", [P, 1], I32)
        nkey = sb("nkey", [P, 1], I32)
        across = ctx.enter_context(nc.psum_tensor("across", [P, P], F32))
        s_low, s_init, s_go, s_key, s_wide, s_acr, s_base, s_calc, s_rank, s_put, s_ea, s_re = (
            sem(n) for n in ("lower_rdy", "place_set", "batch_go", "key_rdy", "wide_rdy", "across_rdy", "base_in", "calc",
                             "rank_rdy", "put", "ea_in", "reloaded"))
        s_low0, s_next = sem("lower_set"), sem("next_put")
        block = ctx.enter_context(nc.Block())
        full, rest = full_rows(EW)
        PUTS = 4

        def columns(eng, body):
            with eng.Fori(0, rest) as t:
                body(t, True)
            with eng.Fori(rest, EW) as t:
                body(t, False)

        @block.sync
        def _(sp):
            with sp.If(sp.value_load(m.unsorted[0:1, 0:1]) != 0):
                sp.dma_start(m.place.rearrange("(a b) -> a b", b=CB), m.ends[0:CPAD].rearrange("(a b) -> a b", b=CB))\
                    .then_inc(s_init, 16)
                ea_cols = m.ea[0:full * EW, :].rearrange("(p t) f -> t p f", t=EW)

                def features(t, more):
                    sp.wait_ge(s_go, t + 1)
                    sp.nop(nofuse=True)
                    sp.dma_start(one_ea[0:full, :], ea_cols[bass.ds(t, 1), :, :].rearrange("o p f -> (o p) f"))\
                        .then_inc(s_ea, 16)
                    if more:
                        sp.dma_start(one_ea[full:full + 1, :], m.ea[bass.ds(t + full * EW, 1), :]).then_inc(s_ea, 16)

                columns(sp, features)
                sp.wait_ge(s_go, EW + 1)
                for buf, arr in ((m.dst_sb, m.dst_s), (m.src_sb, m.src_s), (m.w_sb, m.w_s)):
                    sp.dma_start(buf[:, :], arr.rearrange("(p e) -> p e", e=EW)).then_inc(s_re, 16)
                with nc.allow_non_contiguous_dma(reason="one neighbour per partition"):
                    sp.dma_start(m.before[1:P, :],
                                 m.dst_s[0:EP - EW].rearrange("(p e) -> p e", e=EW)[:, EW - 1:EW]).then_inc(s_re, 16)
                n = load_source_order(nc, m, sp, s_re, m.src_s, True)
                sp.wait_ge(s_re, 64 + n)

        @block.gpsimd
        def _(g):
            with g.If(g.value_load(m.unsorted[0:1, 0:1]) != 0):
                nc.gpsimd.memset(lower[:, :], 1.0).then_inc(s_low0, 1)
                nc.gpsimd.memset(one_ea[:, :], 0.0).then_inc(s_low0, 1)
                g.wait_ge(s_low0, 2)
                nc.gpsimd.affine_select(out=lower[:, :], in_=lower[:, :], compare_op=ALU.is_gt, fill=0.0, base=0,
                                        pattern=[[-1, P]], channel_multiplier=1).then_inc(s_low, 1)
                g.wait_ge(s_init, 16)
                g.wait_ge(s_low, 1)
                g.sem_inc(s_go, 1)

                def put(t, more):
                    g.wait_ge(s_key, t + 1)
                    g.nop(nofuse=True)
                    g.indirect_dma_start(base[:, :], None, m.place.unsqueeze(1),
                                         bass.IndirectOffsetOnAxis(ap=key[:, :], axis=0)).then_inc(s_base, 16)
                    g.wait_ge(s_ea, (t + 1) * 32 if more else t * 16 + (rest + 1) * 16)
                    g.nop(nofuse=True)
                    g.wait_ge(s_rank, t + 1)
                    g.nop(nofuse=True)
                    for table, buf in ((m.src_s.unsqueeze(1), one_src), (m.dst_s.unsqueeze(1), key),
                                       (m.w_s.unsqueeze(1), one_w), (m.ea_s, one_ea)):
                        g.indirect_dma_start(table, bass.IndirectOffsetOnAxis(ap=rank[:, :], axis=0), buf[:, :], None)\
                            .then_inc(s_put, 16)
                    g.indirect_dma_start(m.place.unsqueeze(1), bass.IndirectOffsetOnAxis(ap=nkey[:, :], axis=0), nxt[:, :],
                                         None, bounds_check=CPAD - 1, oob_is_err=False).then_inc(s_next, 16)
                    g.wait_ge(s_put, (t + 1) * 16 * PUTS)
                    g.nop(nofuse=True)
                    g.wait_ge(s_next, (t + 1) * 16)
                    g.nop(nofuse=True)
                    g.sem_inc(s_go, 1)

                columns(g, put)

        @block.vector
        def _(v):
            with v.If(v.value_load(m.unsorted[0:1, 0:1]) != 0):
                STEPS_V = 7

                def rank_batch(t, more):
                    count = [0]

                    def link(ins):
                        count[0] += 1
                        ins.then_inc(s_calc, 1)
                        v.wait_ge(s_calc, t * STEPS_V + count[0])

                    v.wait_ge(s_go, t + 1)
                    col = bass.ds(t, 1)
                    link(nc.vector.tensor_copy(wide[:, :], m.dst_sb[:, col].to_broadcast([P, P])))
                    v.sem_inc(s_wide, 1)
                    nc.vector.tensor_copy(one_src[:, :], m.src_sb[:, col])
                    nc.vector.tensor_copy(one_w[:, :], m.w_sb[:, col])
                    nc.vector.tensor_copy(key[:, :], m.dst_sb[:, col]).then_inc(s_key, 1)
                    v.wait_ge(s_acr, t + 1)
                    link(nc.vector.tensor_scalar(same[:, :], across[:, :], wide[:, 0:1], None, ALU.is_equal))
                    link(nc.vector.reduce_sum(total[:, :], same[:, :], AX.X))
                    link(nc.vector.tensor_tensor(sameb[:, :], same[:, :], lower[:, :], ALU.mult))
                    link(nc.vector.reduce_sum(prior[:, :], sameb[:, :], AX.X))
                    v.wait_ge(s_base, (t + 1) * 16)
                    nc.vector.tensor_tensor(rank[:, :], base[:, :], prior[:, :], ALU.add)
                    nc.vector.tensor_tensor(nxt[:, :], base[:, :], total[:, :], ALU.add)
                    link(nc.vector.tensor_tensor(skip[:, :], total[:, :], prior[:, :], ALU.subtract))
                    link(nc.vector.tensor_scalar(skip[:, :], skip[:, :], -1.0, SKIP, ALU.add, ALU.mult))
                    nc.vector.tensor_tensor(nkey[:, :], skip[:, :], wide[:, 0:1], ALU.add).then_inc(s_rank, 1)
                    assert count[0] == STEPS_V

                columns(v, rank_batch)

        @block.tensor
        def _(pe):
            with pe.If(pe.value_load(m.unsorted[0:1, 0:1]) != 0):
                def turn(t, more):
                    pe.wait_ge(s_wide, t + 1)
                    nc.tensor.transpose(across[:, :], wide[:, :], m.ident[:, :]).then_inc(s_acr, 1)

                columns(pe, turn)


def phase_pack(nc, m):
    with ExitStack() as ctx:
        def sb(name, shape, dt=F32):
            return ctx.enter_context(nc.sbuf_tensor(name, shape, dt))

        def sem(name):
            return ctx.enter_context(nc.semaphore(name))

        part = sb("part2", [P, EW], I32)
        pack = sb("pack", [P, EW, 3])
        flag = sb("flag", [P, EW])
        maskb = sb("maskb", [P, EW], BF16)
        tile_src = sb("tile_src", [P, PE_ROWS])
        turned_src = sb("turned_src", [PE_ROWS, P], mybir.dt.int16)
        ps_src = ctx.enter_context(nc.psum_tensor("ps_src", [PE_ROWS, P], F32))
        s_vec, s_packed, s_mask, s_out = (sem(n) for n in ("vec2", "packed_rdy", "mask_rdy", "stored2"))
        s_tsrc, s_psrc, s_rsrc = (sem(n) for n in ("tile_src_rdy", "tile_src_up", "tile_src_out"))
        block = ctx.enter_context(nc.Block())

        @block.sync
        def _(sp):
            sp.wait_ge(s_packed, 3)
            sp.dma_start(m.packed.rearrange("(p r) c -> p (r c)", p=P),
                         pack[:, :, :].rearrange("p e c -> p (e c)")).then_inc(s_out, 16)
            sp.wait_ge(s_mask, 1)
            sp.dma_start(m.mask, maskb[:, :]).then_inc(s_out, 16)
            sp.wait_ge(s_rsrc, 1)
            sp.dma_start(m.pe_src, turned_src[:, :]).then_inc(s_out, 16)
            sp.wait_ge(s_out, 48)

        @block.tensor
        def _(pe):
            pe.wait_ge(s_tsrc, 1)
            nc.tensor.transpose(ps_src[:, :], tile_src[:, :], m.ident[:, :]).then_inc(s_psrc, 1)

        @block.vector
        def _(v):
            link = Chain(v, s_vec)
            dst, src = m.dst_sb, m.src_sb
            by_slot = m.src_idx[:, :].rearrange("p (h c j) -> p h c j", c=U, j=4)
            for n, k in enumerate(PE_SLOTS):
                c = nc.vector.tensor_copy(tile_src[:, :].rearrange("p (h n) -> p h n", n=len(PE_SLOTS))[:, :, n],
                                          by_slot[:, :, k, PE_TILE])
            c.then_inc(s_tsrc, 1)
            link(nc.vector.tensor_scalar(part[:, :], src[:, :], NB - 1, None, ALU.bitwise_and))
            nc.vector.tensor_copy(pack[:, :, 0], part[:, :]).then_inc(s_packed, 1)
            v.wait_ge(s_packed, 1)
            link(nc.vector.tensor_scalar(part[:, :], src[:, :], 7, None, ALU.arith_shift_right))
            nc.vector.scalar_tensor_tensor(out=pack[:, :, 1], in0=dst[:, :], scalar=float(NA), in1=part[:, :],
                                           op0=ALU.mult, op1=ALU.add).then_inc(s_packed, 1)
            nc.vector.tensor_copy(pack[:, :, 2], m.w_sb[:, :]).then_inc(s_packed, 1)
            link(nc.vector.tensor_tensor(flag[:, 1:EW], dst[:, 1:EW], dst[:, 0:EW - 1], ALU.not_equal))
            link(nc.vector.tensor_tensor(flag[:, 0:1], dst[:, 0:1], m.before[:, :], ALU.not_equal))
            nc.vector.tensor_scalar(maskb[:, :], flag[:, :], FAR, None, ALU.mult).then_inc(s_mask, 1)
            v.wait_ge(s_psrc, 1)
            nc.vector.tensor_copy(turned_src[:, :], ps_src[:, :]).then_inc(s_rsrc, 1)


def phase_adjacency(nc, m):
    BS = 10
    NBT = STEPS // BS
    BP = 5
    BANKS = [4] * 6 + [1]
    NBK = len(BANKS)
    CLOSES = [(HALF * sum(BANKS[:k + 1]) - 1) // BS for k in range(NBK)]
    LAG = 2

    def known(i):
        return isinstance(i, int)

    def over_tiles(eng, w, body):
        if w == 0:
            body(0)
        with eng.Fori(max(w * NP // GK, 1), (w + 1) * NP // GK) as t:
            body(t)

    with ExitStack() as ctx:
        def sb(name, shape, dt=F32):
            return ctx.enter_context(nc.sbuf_tensor(name, shape, dt))

        def sem(name):
            return ctx.enter_context(nc.semaphore(name))

        lo = sb("lo", [NP, GT], I32)
        rowi = sb("rowi", [NP, GT], I32)
        widx = sb("widx", [NP, GT, WR], I32)
        nb = sb("nb", [NP, NT], I32)
        ne = sb("ne", [NP, NT], I32)
        hi = sb("hi", [NP, GT], I32)
        used = sb("used", [NP, GT])
        over = sb("over", [NP, GT])
        overs = sb("overs", [NP, 1])
        has = sb("has", [NP, NT])
        last = sb("last", [NP, NT])
        win = sb("win", [NP, GT, WR * 3 * ROW])
        goff_i = sb("goff_i", [P, NG], I32)
        goff = sb("goff", [P, NG])
        cols = [sb(f"col{c}", [P, NG * HALF], BF16 if c == 0 else F32) for c in range(3)]
        iota_k = sb("iota_k", [P, NB, BS], BF16)
        oh_b = [sb(f"hot_b{r}", [P, NB, BS], BF16) for r in range(NBT)]
        oh_m = [sb(f"hot_m{r}", [P, BS, NP]) for r in range(NBT)]
        oh_w = [sb(f"hot_w{r}", [P, BS, NB]) for r in range(NBT)]
        rows = sb("rows", [NP, 2, GK, NB])
        pt = [ctx.enter_context(nc.psum_tensor(f"pt{k}", [P, 512], F32)) for k in range(8)]

        s_ld, s_dv, s_gidx, s_gidx2 = sem("ends_in"), sem("dve_chain"), sem("goff_rdy"), sem("widx_rdy")
        s_win = [sem(f"win_in{w}") for w in range(GT)]
        turn_bank = pt[7][:, 0:3 * P].rearrange("p (n c) -> p n c", n=3)
        s_over, s_crowd = sem("over_rdy"), sem("crowd_rdy")
        s_tr, s_ev = sem("slots_up"), sem("slots_out")
        s_ohb, s_ohm, s_wp, s_wa, s_used, s_done = (
            sem(n) for n in ("b_onehots", "row_onehots", "pool_weighted", "act_weighted", "batch_used", "bank_done"))
        s_rfree, s_rr = [sem(f"rows_stored{k}") for k in range(2)], sem("rows_rdy")
        block = ctx.enter_context(nc.Block())
        CUT = 112

        @block.sync
        def _(sp):
            with nc.allow_non_contiguous_dma(reason="one count per group or node"):
                sp.dma_start(lo[:, :], m.ends[0:N].rearrange("(t p g) -> p t g", p=NP, g=G)[:, :, 0]).then_inc(s_ld, 16)
                sp.dma_start(hi[:, :], m.ends[G:N + G].rearrange("(t p g) -> p t g", p=NP, g=G)[:, :, 0]).then_inc(s_ld, 16)
                sp.dma_start(nb[:, :], m.ends[0:N].rearrange("(k p) -> p k", p=NP)).then_inc(s_ld, 16)
                sp.dma_start(ne[:, :], m.ends[1:1 + N].rearrange("(k p) -> p k", p=NP)).then_inc(s_ld, 16)
            out = m.adj.rearrange("d (a b) -> (d a) b", b=NB).rearrange("(q m) b -> m q b", m=NP)

            def store(k, t, parity):
                at = t * GK if isinstance(t, int) else sp.snap(t * GK)
                sp.wait_ge(s_rr, (t + 1) * NBK)
                for p0, p1 in ((0, CUT), (CUT, NP)):
                    sp.dma_start(out[p0:p1, bass.ds(at, GK), :],
                                 rows[p0:p1, parity, :, :]).then_inc(s_rfree[parity], 16)

            with sp.Fori(0, NT // 2) as i:
                for k in range(2):
                    store(k, i * 2 + k, k)
            store(0, NT - 1, 0)
            sp.wait_ge(s_rfree[0], 32 * (NT // 2 + 1))
            sp.wait_ge(s_rfree[1], 32 * (NT // 2))

        @block.gpsimd
        def _(g):
            nc.gpsimd.iota(goff_i[:, :], pattern=[[NP, NG]], base=0, channel_multiplier=0).then_inc(s_gidx, 1)
            g.wait_ge(s_gidx2, 1)

            def fetch(w):
                for r in range(WR):
                    g.indirect_dma_start(win[:, w, r * 3 * ROW:(r + 1) * 3 * ROW], None, m.packed,
                                         bass.IndirectOffsetOnAxis(ap=widx[:, w, r:r + 1], axis=0)).then_inc(s_win[w], 16)

            def tile(t):
                for b in range(NBT):
                    n = t * NBT + b
                    g.wait_ge(s_ohb, n + 1)
                    if not known(t) or t > 0:
                        g.wait_ge(s_used, n + 1 - NBT)
                    nc.gpsimd.tensor_tensor(
                        oh_w[b][:, 0:BP, :], oh_b[b][:, :, 0:BP].rearrange("p m k -> p k m"),
                        cols[2][:, bass.ds(t * STEPS + b * BS, BP)].unsqueeze(2).to_broadcast([P, BP, NB]),
                        ALU.mult).then_inc(s_wp, 1)

            fetch(0)
            for w in range(GT):
                if w + 1 < GT:
                    fetch(w + 1)
                over_tiles(g, w, tile)
            for w in range(GT):
                g.wait_ge(s_win[w], 16 * WR)

        @block.vector
        def _(v):
            link = Chain(v, s_dv)
            v.wait_ge(s_ld, 64)
            link(nc.vector.tensor_scalar(rowi[:, :], lo[:, :], 5, None, ALU.arith_shift_right))
            for r in range(WR):
                w = nc.vector.tensor_scalar(widx[:, :, r], rowi[:, :], float(r), None, ALU.add)
            w.then_inc(s_gidx2, 1)
            link(nc.vector.tensor_scalar(used[:, :], rowi[:, :], float(-ROW), None, ALU.mult))
            link(nc.vector.tensor_tensor(used[:, :], used[:, :], hi[:, :], ALU.add))
            link(nc.vector.tensor_scalar(over[:, :], used[:, :], float(WIN), None, ALU.is_gt))
            nc.vector.reduce_sum(overs[:, :], over[:, :], AX.X).then_inc(s_over, 1)
            zero_row = float(NC * CH)
            link(nc.vector.tensor_tensor(has[:, :], ne[:, :], nb[:, :], ALU.is_gt))
            link(nc.vector.tensor_scalar(last[:, :], ne[:, :], -1.0 - zero_row, None, ALU.add))
            link(nc.vector.tensor_tensor(last[:, :], last[:, :], has[:, :], ALU.mult))
            link(nc.vector.tensor_scalar(m.end_idx[:, :], last[:, :], zero_row, None, ALU.add))
            v.wait_ge(s_crowd, 1)
            link(nc.vector.tensor_copy(m.crowded[:, :], pt[6][0:1, 0:1]))
            v.wait_ge(s_gidx, 1)
            link(nc.vector.tensor_copy(goff[:, :], goff_i[:, :]))
            link(nc.vector.tensor_copy(iota_k[:, :, :], m.iota[:, :].unsqueeze(2).to_broadcast([P, NB, BS])))

            def slots_out(w):
                for h in range(HALF):
                    n = (w * HALF + h + 1) * 3
                    v.wait_ge(s_tr, n)
                    for c in range(3):
                        out = cols[c][:, :].rearrange("p (t q h) -> p t h q", t=GT, h=HALF)[:, w, h, :]
                        up = turn_bank[:, c, 0:NP]
                        if c == 1:
                            nc.vector.tensor_tensor(out, up, goff[:, w * NP:(w + 1) * NP], ALU.subtract).then_inc(s_ev, 1)
                        else:
                            nc.vector.tensor_copy(out, up).then_inc(s_ev, 1)
                v.wait_ge(s_ev, n)

            def tile(t):
                for b in range(NBT):
                    n = t * NBT + b
                    steps = bass.ds(t * STEPS + b * BS, BS)
                    if not known(t) or t > 0:
                        v.wait_ge(s_used, n + 1 - NBT)
                    nc.vector.tensor_tensor(oh_b[b][:, :, :], iota_k[:, :, :],
                                            cols[0][:, steps].unsqueeze(1).to_broadcast([P, NB, BS]),
                                            ALU.is_equal).then_inc(s_ohb, 1)
                    nc.vector.tensor_tensor(oh_m[b][:, :, :], m.iota[:, 0:NP].unsqueeze(1).to_broadcast([P, BS, NP]),
                                            cols[1][:, steps].unsqueeze(2).to_broadcast([P, BS, NP]),
                                            ALU.is_equal).then_inc(s_ohm, 1)

            for w in range(GT):
                slots_out(w)
                over_tiles(v, w, tile)

        @block.scalar
        def _(act):
            def weight(t, b):
                n = t * NBT + b
                act.wait_ge(s_ohb, n + 1)
                if not known(t) or t > 0:
                    act.wait_ge(s_used, n + 1 - NBT)
                for k in range(BP, BS):
                    w = nc.scalar.mul(oh_w[b][:, k, :], oh_b[b][:, :, k], cols[2][:, bass.ds(t * STEPS + b * BS + k, 1)])
                w.then_inc(s_wa, 1)

            def copy_out(t, parity, turn, b):
                for k in range(NBK):
                    if CLOSES[k] != b:
                        continue
                    if k == 0 and (not known(turn) or turn > 0):
                        act.wait_ge(s_rfree[parity], turn * 32)
                    act.wait_ge(s_done, t * NBK + k + 1)
                    q, n = sum(BANKS[:k]), BANKS[k]
                    nc.scalar.copy(rows[:, parity, q:q + n, :], pt[k][0:NP, 0:n * NB].rearrange("p (q b) -> p q b", b=NB))\
                        .then_inc(s_rr, 1)

            def two_tiles(turn, tiles):
                for parity in range(tiles):
                    t = turn * 2 + parity
                    for b in range(NBT):
                        weight(t, b)
                        if b >= LAG:
                            copy_out(t, parity, turn, b - LAG)
                        elif parity:
                            copy_out(t - 1, 0, turn, b + NBT - LAG)
                        elif not known(turn) or turn > 0:
                            copy_out(t - 1, 1, turn - 1, b + NBT - LAG)

            two_tiles(0, 2)
            with act.Fori(1, NT // 2) as i:
                two_tiles(i, 2)
            two_tiles(NT // 2, 1)
            for b in range(NBT - LAG, NBT):
                copy_out(NT - 1, 0, NT // 2, b)

        @block.tensor
        def _(pe):
            pe.wait_ge(s_over, 1)
            nc.tensor.matmul(pt[6][0:1, 0:1], overs[:, :], m.ones[0:NP, :], start=True, stop=True).then_inc(s_crowd, 1)

            def turn_slots(w):
                parts = win[:, w, :].rearrange("p (s c) -> p c s", c=3)
                pe.wait_ge(s_win[w], 16 * WR)
                for h in range(HALF):
                    if w * HALF + h > 0:
                        pe.wait_ge(s_ev, (w * HALF + h) * 3)
                    for c in range(3):
                        nc.tensor.transpose(turn_bank[:, c, 0:NP], parts[:, c, P * h:P * h + P],
                                            m.ident[0:NP, 0:NP]).then_inc(s_tr, 1)

            def tile(t):
                for k, groups in enumerate(BANKS):
                    if not known(t) or t > 0:
                        pe.wait_ge(s_rr, (t - 1) * NBK + k + 1)
                    for s in range(HALF * sum(BANKS[:k]), HALF * sum(BANKS[:k + 1])):
                        b, j, q, h = s // BS, s % BS, s // HALF - sum(BANKS[:k]), s % HALF
                        if j == 0:
                            pe.wait_ge(s_ohm, t * NBT + b + 1)
                            pe.wait_ge(s_wp, t * NBT + b + 1)
                            pe.wait_ge(s_wa, t * NBT + b + 1)
                        mm = nc.tensor.matmul(pt[k][0:NP, q * NB:(q + 1) * NB], oh_m[b][:, j, :], oh_w[b][:, j, :],
                                              start=h == 0, stop=h == HALF - 1)
                        closes_bank = s == HALF * sum(BANKS[:k + 1]) - 1
                        if j == BS - 1:
                            mm.then_inc(s_used, 1)
                            if closes_bank:
                                pe.wait_ge(s_used, t * NBT + b + 1)
                                pe.sem_inc(s_done, 1)
                        elif closes_bank:
                            mm.then_inc(s_done, 1)

            for w in range(GT):
                turn_slots(w)
                over_tiles(pe, w, tile)


def phase_crowded(nc, m):
    with ExitStack() as ctx:
        def sb(name, shape, dt=F32):
            return ctx.enter_context(nc.sbuf_tensor(name, shape, dt))

        def sem(name):
            return ctx.enter_context(nc.semaphore(name))

        blank = sb("blank", [NP, SPAD])
        spot = sb("spot", [P, EW])
        upper = sb("upper", [P, P])
        wide = sb("wide_k", [P, P])
        wide_w = sb("wide_w", [P, P])
        same = sb("same_k", [P, P])
        later = sb("later", [P, P])
        share = sb("share", [P, P])
        key = sb("key_k", [P, 1], I32)
        nkey = sb("nkey_k", [P, 1], I32)
        old = sb("old", [P, 1])
        new = sb("new", [P, 1])
        sums = sb("sums", [P, 1])
        skip = sb("skip_k", [P, 1])
        across = ctx.enter_context(nc.psum_tensor("across_k", [P, P], F32))
        across_w = ctx.enter_context(nc.psum_tensor("across_w", [P, P], F32))
        s_up0, s_up, s_blank, s_zero, s_go, s_key, s_wide, s_acr, s_old, s_calc, s_new, s_put, s_dv = (
            sem(n) for n in ("upper_set", "upper_rdy", "blank_rdy", "zeroed", "batch_go_k", "key_rdy_k", "wide_rdy_k",
                             "across_rdy_k", "old_in", "calc_k", "new_rdy", "put_k", "spot_chain"))
        block = ctx.enter_context(nc.Block())
        CELLS = N * SPAD
        cells = m.adj.rearrange("d s -> (d s)").unsqueeze(1)

        @block.sync
        def _(sp):
            with sp.If(sp.value_load(m.crowded[0:1, 0:1]) != 0):
                sp.wait_ge(s_blank, 1)
                for k in range(NT):
                    sp.dma_start(m.adj[k * NP:(k + 1) * NP, :], blank[:, :]).then_inc(s_zero, 16)
                sp.wait_ge(s_zero, 16 * NT)

        @block.gpsimd
        def _(g):
            with g.If(g.value_load(m.crowded[0:1, 0:1]) != 0):
                nc.gpsimd.memset(upper[:, :], 1.0).then_inc(s_up0, 1)
                g.wait_ge(s_up0, 1)
                nc.gpsimd.affine_select(out=upper[:, :], in_=upper[:, :], compare_op=ALU.is_gt, fill=0.0, base=0,
                                        pattern=[[1, P]], channel_multiplier=-1).then_inc(s_up, 1)
                g.wait_ge(s_up, 1)
                g.wait_ge(s_zero, 16 * NT)
                g.sem_inc(s_go, 1)
                with g.Fori(0, EW) as t:
                    g.wait_ge(s_key, t + 1)
                    g.nop(nofuse=True)
                    g.indirect_dma_start(old[:, :], None, cells,
                                         bass.IndirectOffsetOnAxis(ap=key[:, :], axis=0)).then_inc(s_old, 16)
                    g.wait_ge(s_new, t + 1)
                    g.nop(nofuse=True)
                    g.indirect_dma_start(cells, bass.IndirectOffsetOnAxis(ap=nkey[:, :], axis=0), new[:, :], None,
                                         bounds_check=CELLS - 1, oob_is_err=False).then_inc(s_put, 16)
                    g.wait_ge(s_put, (t + 1) * 16)
                    g.nop(nofuse=True)
                    g.sem_inc(s_go, 1)

        @block.vector
        def _(v):
            with v.If(v.value_load(m.crowded[0:1, 0:1]) != 0):
                first = Chain(v, s_dv)
                nc.vector.memset(blank[:, :], 0.0).then_inc(s_blank, 1)
                first(nc.vector.scalar_tensor_tensor(out=spot[:, :], in0=m.dst_sb[:, :], scalar=float(SPAD),
                                                     in1=m.src_sb[:, :], op0=ALU.mult, op1=ALU.add))
                first(nc.vector.tensor_scalar(spot[:, :], spot[:, :], float(CELLS - 1), None, ALU.min))
                STEPS_V = 9
                with v.Fori(0, EW) as t:
                    count = [0]

                    def link(ins):
                        count[0] += 1
                        ins.then_inc(s_calc, 1)
                        v.wait_ge(s_calc, t * STEPS_V + count[0])

                    v.wait_ge(s_go, t + 1)
                    col = bass.ds(t, 1)
                    link(nc.vector.tensor_copy(wide[:, :], spot[:, col].to_broadcast([P, P])))
                    link(nc.vector.tensor_copy(wide_w[:, :], m.w_sb[:, col].to_broadcast([P, P])))
                    v.sem_inc(s_wide, 1)
                    nc.vector.tensor_copy(key[:, :], spot[:, col]).then_inc(s_key, 1)
                    v.wait_ge(s_acr, (t + 1) * 2)
                    link(nc.vector.tensor_scalar(same[:, :], across[:, :], wide[:, 0:1], None, ALU.is_equal))
                    link(nc.vector.tensor_tensor(share[:, :], same[:, :], across_w[:, :], ALU.mult))
                    link(nc.vector.reduce_sum(sums[:, :], share[:, :], AX.X))
                    link(nc.vector.tensor_tensor(later[:, :], same[:, :], upper[:, :], ALU.mult))
                    link(nc.vector.reduce_sum(skip[:, :], later[:, :], AX.X))
                    link(nc.vector.tensor_scalar(skip[:, :], skip[:, :], SKIP, None, ALU.mult))
                    v.wait_ge(s_old, (t + 1) * 16)
                    link(nc.vector.tensor_tensor(new[:, :], old[:, :], sums[:, :], ALU.add))
                    nc.vector.tensor_tensor(nkey[:, :], skip[:, :], wide[:, 0:1], ALU.add).then_inc(s_new, 1)
                    assert count[0] == STEPS_V

        @block.tensor
        def _(pe):
            with pe.If(pe.value_load(m.crowded[0:1, 0:1]) != 0):
                with pe.Fori(0, EW) as t:
                    pe.wait_ge(s_wide, t + 1)
                    nc.tensor.transpose(across[:, :], wide[:, :], m.ident[:, :]).then_inc(s_acr, 1)
                    nc.tensor.transpose(across_w[:, :], wide_w[:, :], m.ident[:, :]).then_inc(s_acr, 1)


def layer_norm(nc, link, x, tmp, stats, out, s_var, s_root, v, n=1):
    shape = list(x.shape)
    mean, var = stats[:, 0, :], stats[:, 1, :]
    link(nc.vector.reduce_sum(mean, x, AX.X))
    link(nc.vector.tensor_scalar(mean, mean, 1.0 / D, None, ALU.mult))
    link(nc.vector.tensor_tensor(x, x, mean.unsqueeze(2).to_broadcast(shape), ALU.subtract))
    link(nc.vector.tensor_tensor(tmp, x, x, ALU.mult))
    link(nc.vector.reduce_sum(var, tmp, AX.X))
    nc.vector.tensor_scalar(var, var, 1.0 / D, None, ALU.mult).then_inc(s_var, 1)
    v.wait_ge(s_root, n)
    link(nc.vector.reciprocal(var, var))
    link(nc.vector.tensor_tensor(out, x, var.unsqueeze(2).to_broadcast(shape), ALU.mult))


def phase_propagate(nc, m):
    with ExitStack() as ctx:
        def sb(name, shape, dt=F32):
            return ctx.enter_context(nc.sbuf_tensor(name, shape, dt))

        def sem(name):
            return ctx.enter_context(nc.semaphore(name))

        UK = 5
        TURNS = NT // UK
        ego = sb("ego", [NP, NT, D])
        acc = sb("acc", [NP, NT, D])
        tmp = sb("tmp", [NP, NT, D])
        stats = sb("stats", [NP, 2, NT])
        slot = [sb(f"slot{k}", [NP, D]) for k in range(UK)]
        at = [sb(f"at{k}", [NP, N]) for k in range(UK)]
        kept = [sb(f"kept{k}", [NP, N]) for k in range(UK)]
        agg_t = sb("agg_t", [D, N])
        pa = [ctx.enter_context(nc.psum_tensor(f"pa{k}", [P, 512], F32)) for k in range(8)]
        s_at = [sem(f"adj_in{k}") for k in range(UK)]
        s_afree, s_init, s_slot, s_agg, s_out, s_tr, s_upd, s_ln, s_rt, s_dv = (
            sem(n) for n in ("adj_free", "ego_init", "slot_rdy", "agg_done", "agg_out", "turned", "updated", "ln_var", "ln_root",
                             "dve_chain2"))
        s_kept = sem("kept_in")
        FREE0 = 2 * UK
        block = ctx.enter_context(nc.Block())
        SEG = [(512 * b, min(512, N - 512 * b)) for b in range(-(-N // 512))]
        TB = 5

        @block.sync
        def _(sp):
            with sp.Fori(0, ROUNDS) as r:
                for k in range(UK):
                    sp.wait_ge(s_afree, r * NT + k + 1 - 2 * UK + FREE0)
                    for p0, p1 in ((0, 112), (112, NP)):
                        sp.dma_start(at[k][p0:p1, :], m.adj[k * NP + p0:k * NP + p1, 0:N]).then_inc(s_at[k], 16)
                with sp.Fori(1, TURNS - 1) as i:
                    for k in range(UK):
                        rows = [(sp.snap((i * UK + k) * NP + p0), p0, p1) for p0, p1 in ((0, 112), (112, NP))]
                        sp.wait_ge(s_afree, r * NT + i * UK + k + 1 - UK + FREE0)
                        for row, p0, p1 in rows:
                            sp.dma_start(at[k][p0:p1, :], m.adj[bass.ds(row, p1 - p0), 0:N]).then_inc(s_at[k], 16)

        @block.gpsimd
        def _(g):
            for k in range(UK):
                for p0, p1 in ((0, 112), (112, NP)):
                    g.dma_start(kept[k][p0:p1, :], m.adj[(NT - UK + k) * NP + p0:(NT - UK + k) * NP + p1, 0:N])\
                        .then_inc(s_kept, 16)
            g.wait_ge(s_kept, 32 * UK)

        @block.vector
        def _(v):
            link = Chain(v, s_dv)
            link(nc.vector.tensor_copy(ego[:, :, :], m.x[:, :, :]))
            link(nc.vector.tensor_copy(acc[:, :, :], m.x[:, :, :]))
            with v.Fori(0, ROUNDS) as r:
                with v.Fori(0, NT // UK) as i:
                    for k in range(UK):
                        n = r * NT + i * UK + k
                        v.wait_ge(s_afree, n + 1 - UK + FREE0)
                        nc.vector.tensor_copy(slot[k][:, :], ego[:, bass.ds(i * UK + k, 1), :].rearrange("p a d -> p (a d)"))\
                            .then_inc(s_slot, 1)
                for b in range(NT // TB):
                    v.wait_ge(s_tr, r * (NT // TB) + b + 1)
                    e = ego[:, b * TB:(b + 1) * TB, :]
                    g = pa[b][0:NP, 0:TB * D].rearrange("p (k d) -> p k d", d=D)
                    nc.vector.scalar_tensor_tensor(out=e, in0=e, scalar=1.0, in1=g, op0=ALU.add, op1=ALU.mult)\
                        .then_inc(s_upd, 1)
                v.wait_ge(s_upd, (r * 2 + 1) * (NT // TB))
                for b in range(NT // TB):
                    e, a = (t[:, b * TB:(b + 1) * TB, :] for t in (ego, acc))
                    nc.vector.tensor_tensor(a, a, e, ALU.add).then_inc(s_upd, 1)
                v.wait_ge(s_upd, (r + 1) * 2 * (NT // TB))
            link(nc.vector.scalar_tensor_tensor(out=acc[:, :, :], in0=acc[:, :, :], scalar=1.0 / (ROUNDS + 1),
                                                in1=m.x[:, :, :], op0=ALU.mult, op1=ALU.add))
            layer_norm(nc, link, acc[:, :, :], tmp[:, :, :], stats[:, :, :], m.x[:, :, :], s_ln, s_rt, v)

        @block.scalar
        def _(act):
            with act.Fori(0, ROUNDS) as r:
                for b, (c0, w) in enumerate(SEG):
                    act.wait_ge(s_agg, r * len(SEG) + b + 1)
                    nc.scalar.copy(agg_t[:, c0:c0 + w], pa[b][0:D, 0:w]).then_inc(s_out, 1)
            act.wait_ge(s_ln, 1)
            nc.scalar.activation(stats[:, 1, :], stats[:, 1, :], ACT.Sqrt, bias=m.eps[:, :]).then_inc(s_rt, 1)

        @block.tensor
        def _(pe):
            pe.sem_inc(s_afree, FREE0)

            def turn(r, i, first):
                for k in range(UK):
                    pe.wait_ge(s_slot, r * NT + i * UK + k + 1)
                    pe.wait_ge(s_at[k], (r * (TURNS - 1) + i + 1) * 32)
                    for b, (c0, w) in enumerate(SEG):
                        mm = nc.tensor.matmul(pa[b][0:D, 0:w], slot[k][:, :], at[k][:, c0:c0 + w],
                                              start=first and k == 0, stop=False)
                    mm.then_inc(s_afree, 1)

            with pe.Fori(0, ROUNDS) as r:
                turn(r, 0, True)
                with pe.Fori(1, TURNS - 1) as i:
                    turn(r, i, False)
                for k in range(UK):
                    pe.wait_ge(s_slot, (r + 1) * NT - UK + k + 1)
                pe.wait_ge(s_kept, 32 * UK)
                for b, (c0, w) in enumerate(SEG):
                    for k in range(UK):
                        mm = nc.tensor.matmul(pa[b][0:D, 0:w], slot[k][:, :], kept[k][:, c0:c0 + w], start=False,
                                              stop=k == UK - 1)
                    mm.then_inc(s_agg, 1)
                pe.wait_ge(s_agg, (r + 1) * len(SEG))
                pe.sem_inc(s_afree, UK)
                for b in range(NT // TB):
                    pe.wait_ge(s_out, r * len(SEG) + ((b + 1) * TB * NP - 1) // 512 + 1)
                    for j in range(TB):
                        t = b * TB + j
                        mm = nc.tensor.transpose(pa[b][0:NP, j * D:(j + 1) * D], agg_t[:, t * NP:(t + 1) * NP],
                                                 m.ident[0:D, 0:D])
                    mm.then_inc(s_tr, 1)
                pe.wait_ge(s_upd, (r * 2 + 1) * (NT // TB))


CONV_SEMS = ("w_zero", "xt_up", "xt_out", "y_up", "y_out", "idx_staged", "ea_up", "eat_rdy", "feat_up",
             "rows_up", "msg_rdy", "scanned", "maxima_up", "maxima_out", "y_parts_rdy", "hot_rdy", "pe_rows_up",
             "pe_rows_out", "two_parts", "pe_rows_rdy", "all_stored", "chain")


def phase_clear(nc, sems):
    numbers = sorted(s.num for s in sems.values())
    assert numbers[-1] - numbers[0] == len(numbers) - 1
    block_ctx = nc.Block()
    with block_ctx as block:
        @block.sync
        def _(sp):
            sp.sem_clear(range(numbers[0], numbers[-1] + 1))


def phase_conv(nc, m, layer, sems, x_in, w_msg, w_edge, w_root, bias, conv_out, final):
    with ExitStack() as ctx:
        def sb(name, shape, dt=F32):
            return ctx.enter_context(nc.sbuf_tensor(f"{name}_{layer}", shape, dt))

        def sem(name):
            return ctx.enter_context(nc.semaphore(f"{name}_{layer}"))

        L = len(PE_SLOTS)
        V = 2
        wmr = sb("wmr", [D, 2 * D])
        we = sb("we", [P, 4, D])
        bb = sb("bb", [NP, D])
        xt = sb("xt", [D, N])
        y_sb = sb("y_sb", [NP, NT, D])
        z = sb("z", [NP, NT, D])
        agg = sb("agg", [NP, NT, D])
        tmp = sb("tmp", [NP, NT, D])
        stats = sb("stats", [NP, 2, NT])
        gi = [sb(f"gi{k}", [P, 4], I32) for k in range(U)]
        got = [sb(f"got{k}", [P, 4, D]) for k in range(U)]
        ea = [sb(f"ea{k}", [P, 4 * DE]) for k in range(U)]
        eat = [sb(f"eat{k}", [P, P]) for k in range(V)]
        mk = [sb(f"mk{k}", [D, CH], BF16) for k in range(U)]
        sc = [sb(f"sc{k}", [D, CH]) for k in range(U)]
        so = [sb(f"so{k}", [P, 4, D]) for k in range(V)]
        y_parts = sb("y_parts", [NP, NT, 3, D], BF16)
        hot = [sb(f"hot{k}", [NP, NT, P], BF16) for k in range(L)]
        parts = [sb(f"parts{k}", [P, 3 * D]) for k in range(L)]
        msg = [sb(f"msg{k}", [P, 4, D]) for k in range(V)]

        def banks(name, n):
            return [ctx.enter_context(nc.psum_tensor(f"{name}{k}_{layer}", [P, 512], F32)) for k in range(n)]

        ps_f, ps_r, ps_e, ps_g, ps_o = banks("ps_f", V), banks("ps_r", V), banks("ps_e", 1)[0], banks("ps_g", 1)[0], banks("ps_o", V)
        s_wn, s_wl, s_ys = sem("node_w_in"), sem("edge_w_in"), sem("y_stored")
        TG = 5
        s_agg = [sem(f"agg_in{g}") for g in range(NT // TG)]
        s_got = [sem(f"rows_in{k}") for k in range(U)]
        s_in = [sem(f"chunk_in{k}") for k in range(U)]
        s_sw = [sem(f"seg_stored{k}") for k in range(V)]
        (s_wz, s_t, s_te, s_y, s_ye, s_idx, s_eup, s_eat, s_fup, s_rup, s_msg, s_scan, s_up, s_so, s_yp, s_hot,
         s_pg, s_gout, s_sum1, s_sum, s_end, s_dv) = (sems[n] for n in CONV_SEMS)
        if final:
            s_ln, s_rt, s_res, s_out = (sem(n) for n in ("var", "root", "result", "result_out"))
        else:
            s_tab = sem("tables_rdy")
        mask_c = m.mask.rearrange("p e -> (p e)")
        LAG = 2
        LOOPS = NC // U - 1

        def over_chunks(eng, body):
            for k in range(U):
                body(0, k)
            with eng.Fori(1, LOOPS) as i:
                for k in range(U):
                    body(i, k)
            for c in range(LOOPS * U, NC):
                body(c // U, c % U)

        def step(i, k, ahead):
            k += ahead
            return i + k // U, k % U

        def known(i):
            return isinstance(i, int)

        def gathers(k):
            return [j for j in range(4) if k not in PE_SLOTS or j != PE_TILE]

        def turn_of(i, k):
            return i * L + PE_SLOTS.index(k), PE_SLOTS.index(k)

        def has_pe_tile(i, k):
            return k in PE_SLOTS and exists(i, k)

        def arrived(i, k):
            return (i + 1) * 32 + (16 if known(i) and i * U + k == NC - 1 else 0)

        def exists(i, k):
            return not known(i) or i * U + k < NC

        TX = 4
        YG = 5
        XT, YT = -(-NT // TX), NT // YG
        xt_bank = ps_f + ps_r
        y_bank = ps_o + [ps_e, ps_g]
        z_bank = xt_bank + [ps_o[1]]
        block = ctx.enter_context(nc.Block())

        @block.sync
        def _(sp):
            sp.dma_start(wmr[:, 0:D], w_msg).then_inc(s_wn, 16)
            sp.dma_start(wmr[:, D:2 * D], w_root).then_inc(s_wn, 16)
            sp.dma_start(bb[:, :], bias.unsqueeze(0).to_broadcast([NP, D])).then_inc(s_wl, 16)
            sp.wait_ge(s_wz, 1)
            for j in range(4):
                sp.dma_start(we[j * DE:(j + 1) * DE, j, :], w_edge).then_inc(s_wl, 16)

            if not final:
                for p0, p1 in ((0, 112), (112, NP)):
                    sp.dma_start(m.pe_srcs[p0:p1, :], m.pe_src.rearrange("h e -> (h e)")[0:PE_ROWS * P].unsqueeze(0)
                                 .to_broadcast([p1 - p0, PE_ROWS * P])).then_inc(s_tab, 16)
            y_rows = m.y.rearrange("(k p) d -> p k d", p=NP)
            for t in range(0, NT, YG):
                sp.wait_ge(s_ye, t // YG + 1)
                sp.dma_start(y_rows[:, t:t + YG, :], y_sb[:, t:t + YG, :]).then_inc(s_ys, 16)

            def load(i, k):
                c = i * U + k
                edge = c * CH if known(i) else sp.snap(c * CH)
                if not known(i) or i > 0:
                    sp.wait_ge(s_scan, c + 1 - U)
                if not known(i) or c < NC - 1:
                    sp.dma_start(ea[k][:, :], m.ea_s[bass.ds(edge, CH), :].rearrange("(p j) f -> p (j f)", j=4))\
                        .then_inc(s_in[k], 16)
                else:
                    n = E - edge
                    sp.dma_start(ea[k][0:n // 4, :], m.ea_s[edge:edge + n // 4 * 4, :].rearrange("(p j) f -> p (j f)", j=4))\
                        .then_inc(s_in[k], 16)
                    sp.dma_start(ea[k][n // 4:n // 4 + 1, 0:n % 4 * DE],
                                 m.ea_s[edge + n // 4 * 4:E, :].rearrange("(o j) f -> o (j f)", o=1)).then_inc(s_in[k], 16)
                sp.dma_start(mk[k][:, :], mask_c[bass.ds(edge, CH)].unsqueeze(0).to_broadcast([D, CH])).then_inc(s_in[k], 16)

            over_chunks(sp, load)
            if final:
                rows = m.out.rearrange("(k p) d -> p k d", p=NP)
                for g in range(NT // TG):
                    t = slice(g * TG, (g + 1) * TG)
                    sp.wait_ge(s_res, g + 1)
                    sp.dma_start(rows[:, t, :], agg[:, t, :]).then_inc(s_out, 16)
                sp.wait_ge(s_out, 16 * (NT // TG))

        @block.gpsimd
        def _(g):
            nc.gpsimd.memset(we[:, :, :], 0.0).then_inc(s_wz, 1)
            if not final:
                nc.gpsimd.iota(m.node[:, :, :], pattern=[[NP, NT], [0, P]], base=0, channel_multiplier=1).then_inc(s_wz, 1)
            g.wait_ge(s_ys, 16 * (NT // YG))

            def gather(i, k):
                g.wait_ge(s_idx, i * U + k + 1)
                g.nop(nofuse=True)
                for j in gathers(k):
                    g.indirect_dma_start(got[k][:, j, :], None, m.y,
                                         bass.IndirectOffsetOnAxis(ap=gi[k][:, j:j + 1], axis=0)).then_inc(s_got[k], 16)

            over_chunks(g, gather)
            g.wait_ge(s_end, 1)
            for t in range(NT):
                g.indirect_dma_start(agg[:, t, :], None, m.seg,
                                     bass.IndirectOffsetOnAxis(ap=m.end_idx[:, t:t + 1], axis=0)).then_inc(s_agg[t // TG], 16)
            for g_in in s_agg:
                g.wait_ge(g_in, 16 * TG)

        @block.vector
        def _(v):
            link = Chain(v, s_dv)

            def stage(i, k):
                nc.vector.tensor_copy(gi[k][:, :], m.src_idx[:, bass.ds((i * U + k) * 4, 4)]).then_inc(s_idx, 1)

            for k in range(U):
                stage(0, k)
            for n in range(YT):
                v.wait_ge(s_y, n + 1)
                nc.vector.tensor_copy(y_sb[:, n * YG:(n + 1) * YG, :],
                                      y_bank[n % 4][0:NP, 0:YG * D].rearrange("p (t d) -> p t d", d=D)).then_inc(s_ye, 1)
            link(nc.vector.memset(sc[U - 1][:, CH - 1:CH], 0.0))
            v.wait_ge(s_ye, YT)
            rest = y_sb
            for part in range(3):
                link(nc.vector.tensor_copy(y_parts[:, :, part, :], rest[:, :, :]))
                if part < 2:
                    link(nc.vector.tensor_tensor(tmp[:, :, :], rest[:, :, :], y_parts[:, :, part, :], ALU.subtract))
                    rest = tmp
            v.sem_inc(s_yp, 1)
            v.wait_ge(s_wl, 16 * 5)
            for n in range(YT):
                v.wait_ge(s_y, YT + n + 1)
                nc.vector.tensor_tensor(z[:, n * YG:(n + 1) * YG, :],
                                        z_bank[n][0:NP, 0:YG * D].rearrange("p (t d) -> p t d", d=D),
                                        bb[:, :].unsqueeze(1).to_broadcast([NP, YG, D]), ALU.add).then_inc(s_ye, 1)
            if not final:
                v.wait_ge(s_tab, 32)
                v.wait_ge(s_wz, 2)

            def find(i, k):
                n, b = turn_of(i, k)
                if not known(i) or n >= L:
                    v.wait_ge(s_pg, n + 1 - L)
                nc.vector.tensor_tensor(hot[b][:, :, :], m.node[:, :, :],
                                        m.pe_srcs[:, bass.ds(n * P, P)].unsqueeze(1).to_broadcast([NP, NT, P]),
                                        ALU.is_equal).then_inc(s_hot, 1)

            def add_parts(i, k):
                n, b = turn_of(i, k)
                row = got[k][:, PE_TILE, :]
                v.wait_ge(s_gout, n + 1)
                nc.vector.tensor_tensor(row, parts[b][:, 0:D], parts[b][:, D:2 * D], ALU.add).then_inc(s_sum1, 1)
                v.wait_ge(s_sum1, n + 1)
                nc.vector.tensor_tensor(row, row, parts[b][:, 2 * D:3 * D], ALU.add).then_inc(s_sum, 1)

            for k in PE_SLOTS:
                find(0, k)

            def add(i, k):
                c = i * U + k
                if has_pe_tile(i, k):
                    add_parts(i, k)
                v.wait_ge(s_fup, c + 1)
                v.wait_ge(s_got[k], (i + 1) * 16 * len(gathers(k)))
                if k in PE_SLOTS:
                    v.wait_ge(s_sum, turn_of(i, k)[0] + 1)
                if not known(i) or c >= V:
                    v.wait_ge(s_rup, c + 1 - V)
                nc.vector.tensor_tensor(msg[k % V][:, :, :], got[k][:, :, :],
                                        ps_f[k % V][:, 0:4 * D].rearrange("p (j d) -> p j d", d=D), ALU.add).then_inc(s_msg, 1)
                v.wait_ge(s_msg, c + 1)
                if exists(i + 1, k):
                    stage(i + 1, k)

            def scan(i, k):
                c = i * U + k
                v.wait_ge(s_rup, c + 1)
                v.wait_ge(s_in[k], arrived(i, k))
                if not known(i) or c > 0:
                    v.wait_ge(s_scan, c)
                if not known(i) or i > 0:
                    v.wait_ge(s_up, c + 1 - U)
                nc.vector.tensor_tensor_scan(sc[k][:, :], mk[k][:, :], ps_r[k % V][0:D, :], sc[k - 1][:, CH - 1:CH],
                                             ALU.add, ALU.max).then_inc(s_scan, 1)
                if exists(*step(i, k, 1)):
                    add(*step(i, k, 1))
                if has_pe_tile(*step(i, k, 5)):
                    find(*step(i, k, 5))

            add(0, 0)
            over_chunks(v, scan)
            for g in range(NT // TG):
                t = slice(g * TG, (g + 1) * TG)
                v.wait_ge(s_agg[g], 16 * TG)
                link(nc.vector.tensor_tensor(z[:, t, :], z[:, t, :], agg[:, t, :], ALU.add))
                res = tmp if final else conv_out
                link(nc.vector.scalar_tensor_tensor(out=res[:, t, :], in0=z[:, t, :], scalar=SLOPE, in1=z[:, t, :],
                                                    op0=ALU.mult, op1=ALU.max))
                if final:
                    link(nc.vector.tensor_tensor(z[:, t, :], tmp[:, t, :], m.x[:, t, :], ALU.add))
                    layer_norm(nc, link, z[:, t, :], tmp[:, t, :], stats[:, :, t], agg[:, t, :], s_ln, s_rt, v, g + 1)
                    v.sem_inc(s_res, 1)

        @block.scalar
        def _(act):
            for n in range(XT):
                c0, c1 = n * TX * NP, min((n + 1) * TX * NP, N)
                act.wait_ge(s_t, n + 1)
                nc.scalar.copy(xt[:, c0:c1], xt_bank[n % 4][0:D, 0:c1 - c0]).then_inc(s_te, 1)

            def features_out(i, k):
                c = i * U + k
                act.wait_ge(s_eup, c + 1)
                if not known(i) or c >= V:
                    act.wait_ge(s_fup, c + 1 - V)
                nc.scalar.copy(eat[k % V][:, :], ps_e[:, 0:P]).then_inc(s_eat, 1)

            def maxima_out(i, k):
                c = i * U + k
                edge = c * CH if known(i) else act.snap(c * CH)
                act.wait_ge(s_up, c + 1)
                if not known(i) or c >= V:
                    act.wait_ge(s_sw[k % V], i * (U // V) * 16 + k // V * 16)
                nc.scalar.copy(so[k % V][:, :, :], ps_o[k % V][:, 0:4 * D].rearrange("p (j d) -> p j d", d=D)).then_inc(s_so, 1)
                act.wait_ge(s_so, c + 1)
                act.dma_start(m.seg[bass.ds(edge, CH), :].rearrange("(p j) d -> p (j d)", j=4),
                              so[k % V][:, :, :].rearrange("p j d -> p (j d)")).then_inc(s_sw[k % V], 16)

            def rows_out(i, k):
                n, b = turn_of(i, k)
                act.wait_ge(s_pg, n + 1)
                if not known(i) or n >= L:
                    act.wait_ge(s_sum, n + 1 - L)
                nc.scalar.copy(parts[b][:, :], ps_g[:, 0:3 * D]).then_inc(s_gout, 1)

            features_out(0, 0)
            features_out(0, 1)
            rows_out(0, PE_SLOTS[0])

            def chunk(i, k):
                if has_pe_tile(*step(i, k, 2)):
                    rows_out(*step(i, k, 2))
                if exists(*step(i, k, 2)):
                    features_out(*step(i, k, 2))
                if not known(i) or i * U + k >= LAG:
                    maxima_out(*step(i, k, -LAG))

            over_chunks(act, chunk)
            for n in range(LAG, 0, -1):
                maxima_out(*step(NC // U, NC % U, -n))
            for k in range(V):
                act.wait_ge(s_sw[k], (NC - k + V - 1) // V * 16)
            act.sem_inc(s_end, 1)
            if final:
                for g in range(NT // TG):
                    var = stats[:, 1, g * TG:(g + 1) * TG]
                    act.wait_ge(s_ln, g + 1)
                    nc.scalar.activation(var, var, ACT.Sqrt, bias=m.eps[:, :]).then_inc(s_rt, 1)

        @block.tensor
        def _(pe):
            def node_products(bank, t, cols):
                return nc.tensor.matmul(bank[0:NP, t % YG * D:(t % YG + 1) * D], xt[:, t * NP:(t + 1) * NP], wmr[:, cols],
                                        start=True, stop=True)

            for n in range(XT + 2):
                if n < XT:
                    if n >= 4:
                        pe.wait_ge(s_te, n - 3)
                    for t in range(n * TX, min((n + 1) * TX, NT)):
                        mm = nc.tensor.transpose(xt_bank[n % 4][0:D, t % TX * NP:(t % TX + 1) * NP], x_in[:, t, :],
                                                 m.ident[0:NP, 0:NP])
                    mm.then_inc(s_t, 1)
                if n >= 2:
                    if n == 2:
                        pe.wait_ge(s_wn, 16 * 2)
                    pe.wait_ge(s_te, n - 1)
                    for t in range((n - 2) * TX, min((n - 1) * TX, NT)):
                        q = t // YG
                        if t % YG == 0 and q >= 4:
                            pe.wait_ge(s_ye, q - 3)
                        mm = node_products(y_bank[q % 4], t, slice(0, D))
                        if t % YG == YG - 1:
                            mm.then_inc(s_y, 1)
            for t in range(NT):
                if t == (NT // YG - 1) * YG:
                    pe.wait_ge(s_ye, 2)
                mm = node_products(z_bank[t // YG], t, slice(D, 2 * D))
                if t % YG == YG - 1:
                    mm.then_inc(s_y, 1)
            pe.wait_ge(s_ye, 2 * YT)
            pe.wait_ge(s_wl, 16 * 5)

            def turn_features(i, k):
                c = i * U + k
                pe.wait_ge(s_in[k], arrived(i, k))
                if not known(i) or c >= 1:
                    pe.wait_ge(s_eat, c)
                nc.tensor.transpose(ps_e[:, 0:P], ea[k][:, :], m.ident[:, :]).then_inc(s_eup, 1)

            def products(i, k):
                c = i * U + k
                pe.wait_ge(s_eat, c + 1)
                if not known(i) or c >= V:
                    pe.wait_ge(s_msg, c + 1 - V)
                nc.tensor.matmul(ps_f[k % V][:, 0:4 * D], eat[k % V][:, :], we[:, :, :].rearrange("p j d -> p (j d)"),
                                 start=True, stop=True).then_inc(s_fup, 1)

            def turn_messages(i, k):
                c = i * U + k
                pe.wait_ge(s_msg, c + 1)
                if not known(i) or c >= V:
                    pe.wait_ge(s_scan, c + 1 - V)
                cols = ps_r[k % V][0:D, :].rearrange("d (p j) -> d j p", j=4)
                for j in range(4):
                    mm = nc.tensor.transpose(cols[:, j, :], msg[k % V][:, j, :], m.ident[:, :])
                mm.then_inc(s_rup, 1)

            def turn_maxima(i, k):
                c = i * U + k
                pe.wait_ge(s_scan, c + 1)
                if not known(i) or c >= V:
                    pe.wait_ge(s_so, c + 1 - V)
                cols = sc[k][:, :].rearrange("d (p j) -> d j p", j=4)
                for j in range(4):
                    mm = nc.tensor.transpose(ps_o[k % V][:, j * D:(j + 1) * D], cols[:, j, :], m.ident[0:D, 0:D])
                mm.then_inc(s_up, 1)

            def gather_rows(i, k):
                n, b = turn_of(i, k)
                pe.wait_ge(s_hot, n + 1)
                if not known(i) or n >= 1:
                    pe.wait_ge(s_gout, n)
                for t in range(NT):
                    mm = nc.tensor.matmul(ps_g[:, 0:3 * D], hot[b][:, t, :],
                                          y_parts[:, t, :, :].rearrange("p c d -> p (c d)"), start=t == 0, stop=t == NT - 1)
                mm.then_inc(s_pg, 1)

            pe.wait_ge(s_yp, 1)
            turn_features(0, 0)
            turn_features(0, 1)
            products(0, 0)
            gather_rows(0, PE_SLOTS[0])

            def chunk(i, k):
                if exists(*step(i, k, 2)):
                    turn_features(*step(i, k, 2))
                turn_messages(i, k)
                if exists(*step(i, k, 1)):
                    products(*step(i, k, 1))
                if not known(i) or i * U + k >= LAG:
                    turn_maxima(*step(i, k, -LAG))
                if has_pe_tile(*step(i, k, 3)):
                    gather_rows(*step(i, k, 3))

            over_chunks(pe, chunk)
            for n in range(LAG, 0, -1):
                turn_maxima(*step(NC // U, NC % U, -n))


def gnn_program(nc, x, src, dst, edge_attr, edge_weight, weights, out):
    with ExitStack() as ctx:
        m = Mem()
        m.x_in, m.src, m.dst, m.ea, m.w, m.out = x, src, dst, edge_attr, edge_weight, out
        persistent(nc, ctx, m)
        phase_count(nc, m)
        phase_sort(nc, m)
        phase_pack(nc, m)
        phase_adjacency(nc, m)
        phase_crowded(nc, m)
        phase_propagate(nc, m)
        c1 = ctx.enter_context(nc.sbuf_tensor("c1", [NP, NT, D], F32))
        m.pe_srcs = ctx.enter_context(nc.sbuf_tensor("pe_srcs", [NP, PE_ROWS * P], mybir.dt.int16))
        m.node = ctx.enter_context(nc.sbuf_tensor("node", [NP, NT, P], mybir.dt.int16))
        sems = {n: ctx.enter_context(nc.semaphore(n)) for n in CONV_SEMS}
        phase_conv(nc, m, 1, sems, m.x, *weights[0:4], c1, False)
        phase_clear(nc, sems)
        phase_conv(nc, m, 2, sems, c1, *weights[4:8], None, True)


_INS = ["x", "src", "dst", "edge_attr_32", "edge_weight",
        "L1_gnn_W1_msg", "L1_gnn_W1_edge", "L1_gnn_W1_root", "L1_gnn_b1",
        "L1_gnn_W2_msg", "L1_gnn_W2_edge", "L1_gnn_W2_root", "L1_gnn_b2"]


def kernel(**inputs):
    import numpy as np
    import concourse.bacc as bacc
    from concourse.bass_utils import run_bass_kernel_spmd as run

    nc = bacc.Bacc("TRN2", target_bir_lowering=False, num_devices=1)
    arrays, args = {}, []
    for name in _INS:
        a = np.ascontiguousarray(inputs[name])
        arrays[f"in_{name}"] = a
        args.append(nc.dram_tensor(f"in_{name}", a.shape, mybir.dt.from_np(a.dtype), kind="ExternalInput").ap())
    out = nc.dram_tensor("out_x", (N, D), F32, kind="ExternalOutput").ap()
    gnn_program(nc, *args[:5], args[5:], out)
    return run(nc, [arrays], core_ids=[0]).results[0]["out_x"]
```
